# Optimizing a Trainium2 kernel written in Bass

```python
import numpy as np
import jax
import jax.numpy as jnp

def _softmax(x, axis=-1):
    return jax.nn.softmax(x, axis=axis)

def _gelu(x):
    return jax.nn.gelu(x, approximate=True)

def _silu(x):
    return jax.nn.silu(x)

def _sigmoid(x):
    return jax.nn.sigmoid(x)

def _layernorm(x, axis=-1, eps=1e-05):
    m = jnp.mean(x, axis=axis, keepdims=True)
    v = jnp.var(x, axis=axis, keepdims=True)
    return (x - m) / jnp.sqrt(v + eps)

def _scatter_add(tgt, idx, src, axis=0):
    return tgt.at[idx].add(src)

def _segment_sum(src, seg, n):
    return jax.ops.segment_sum(src, seg, n)
kernel_name = 'mk_seq_postln_d1_jaxref_r4_8f288c'

def setup_inputs(seed: int=0):
    np.random.seed(seed)
    _w = jnp.asarray

    def _L0_attn_setup():
        import jax, jax.numpy as jnp
        import numpy as np
        B, T, D = (8, 1024, 256)

        def _ssm_scan(a_bc, bx):

            def combine(e1, e2):
                a1, u1 = e1
                a2, u2 = e2
                return (a1 * a2, a2 * u1 + u2)
            _, y = jax.lax.associative_scan(combine, (a_bc, bx), axis=1)
            return y
        key = jax.random.key(seed)
        k_x, k_a, k_b, k_w, k_bo = jax.random.split(key, 5)
        x = jax.random.normal(k_x, (B, T, D), dtype=jnp.float32)
        a = jax.random.normal(k_a, (D,), dtype=jnp.float32) * 0.5
        b = jax.random.normal(k_b, (D,), dtype=jnp.float32)
        w_out = jax.random.normal(k_w, (D, D), dtype=jnp.float32) * (1.0 / np.sqrt(D))
        b_out = jax.random.normal(k_bo, (D,), dtype=jnp.float32) * 0.01
        return {'x': x, 'a': a, 'b': b, 'w_out': w_out, 'b_out': b_out}
    _L0_attn_in = _L0_attn_setup()

    def _L0_ffn_setup():
        import jax, jax.numpy as jnp
        import numpy as np
        N_EXPERTS = 8
        TOP_K = 2
        key = jax.random.key(seed)
        k1, k2, k3, k4 = jax.random.split(key, 4)
        B, T, C, H, E = (2, 512, 256, 1024, N_EXPERTS)
        x = jax.random.normal(k1, (B, T, C), dtype=jnp.float32)
        router_w = jax.random.normal(k2, (E, C), dtype=jnp.float32) * 0.02
        w1 = jax.random.normal(k3, (E, C, H), dtype=jnp.float32) * (1.0 / np.sqrt(C))
        w2 = jax.random.normal(k4, (E, H, C), dtype=jnp.float32) * (1.0 / np.sqrt(H))
        return {'x': x, 'router_w': router_w, 'w1': w1, 'w2': w2}
    _L0_ffn_in = _L0_ffn_setup()
    _d = {'L0_attn_x': _L0_attn_in['x'], 'L0_attn_a': _L0_attn_in['a'], 'L0_attn_b': _L0_attn_in['b'], 'L0_attn_w_out': _L0_attn_in['w_out'], 'L0_attn_b_out': _L0_attn_in['b_out'], 'L0_ffn_router_w': _L0_ffn_in['router_w'], 'L0_ffn_w1': _L0_ffn_in['w1'], 'L0_ffn_w2': _L0_ffn_in['w2']}
    _x0 = _d['L0_attn_x']
    _d['L0_attn_x'] = jax.random.normal(jax.random.fold_in(jax.random.key(seed), 1), (8, 512, 256), dtype=_x0.dtype)
    del _x0
    return _d

def reference(L0_attn_x, L0_attn_a, L0_attn_b, L0_attn_w_out, L0_attn_b_out, L0_ffn_router_w, L0_ffn_w1, L0_ffn_w2):

    def _L0_attn_ref(x, a, b, w_out, b_out):
        import jax, jax.numpy as jnp
        import numpy as np
        B, T, D = (8, 1024, 256)

        def _ssm_scan(a_bc, bx):

            def combine(e1, e2):
                a1, u1 = e1
                a2, u2 = e2
                return (a1 * a2, a2 * u1 + u2)
            _, y = jax.lax.associative_scan(combine, (a_bc, bx), axis=1)
            return y
        ah = jnp.tanh(a)
        bx = b * x
        a_bc = jnp.broadcast_to(ah, x.shape)
        y = _ssm_scan(a_bc, bx)
        return jnp.einsum('btd,ed->bte', y, w_out) + b_out

    def _L0_ffn_ref(x, router_w, w1, w2):
        import jax, jax.numpy as jnp
        import numpy as np
        N_EXPERTS = 8
        TOP_K = 2
        B, T, C = x.shape
        E = N_EXPERTS
        xf = x.reshape(-1, C)
        logits = jnp.einsum('nc,ec->ne', xf, router_w)
        probs = jax.nn.softmax(logits, axis=-1)
        top_w, top_i = jax.lax.top_k(probs, TOP_K)
        top_w = top_w / jnp.sum(top_w, axis=-1, keepdims=True)
        comb = jnp.einsum('nk,nke->ne', top_w, jax.nn.one_hot(top_i, E, dtype=xf.dtype))
        h = jax.nn.gelu(jnp.einsum('nc,ech->enh', xf, w1), approximate=False)
        y = jnp.einsum('enh,ehc->enc', h, w2)
        out = jnp.einsum('ne,enc->nc', comb, y)
        return out.reshape(B, T, C)
    x = L0_attn_x
    x = _layernorm(x + _L0_attn_ref(x, L0_attn_a, L0_attn_b, L0_attn_w_out, L0_attn_b_out), axis=-1)
    x = _layernorm(x + _L0_ffn_ref(x, L0_ffn_router_w, L0_ffn_w1, L0_ffn_w2), axis=-1)
    return x

_drawn_inputs = setup_inputs


def setup_inputs(seed=0):
    import zlib

    import numpy as np

    out = dict(_drawn_inputs(seed))
    spreads = {}
    factors = {}
    for name, (base, spread) in spreads.items():
        noise = np.random.default_rng([zlib.crc32(name.encode()), seed]).standard_normal(out[name].shape)
        drawn = base * np.exp(spread * noise) if base else spread * noise
        out[name] = jnp.asarray(drawn.astype(out[name].dtype))
    for name, factor in factors.items():
        out[name] = (out[name] * factor).astype(out[name].dtype)
    return out
```

```python
from contextlib import ExitStack

import concourse.bass as bass
from concourse import mybir

F32 = mybir.dt.float32
F16 = mybir.dt.float16
BF16 = mybir.dt.bfloat16
I32 = mybir.dt.int32
U32 = mybir.dt.uint32
ALU = mybir.AluOpType
ACT = mybir.ActivationFunctionType
AX = mybir.AxisListType

P = 128
EPS = 1e-5
XS = 2048.0
S_TOP = 16384.0


def later(c):
    return not isinstance(c, int) or c >= 2


def skewed(eng, n, stages):
    deepest = max(lag for lag, _ in stages)
    lo = deepest + 2 + (deepest % 2)
    hi = n - (n - lo) % 2

    def straight(steps):
        for s in steps:
            for lag, stage in stages:
                if 0 <= s - lag < n:
                    stage(s - lag, (s - lag) % 2, (s - lag) // 2)

    straight(range(lo))
    with eng.Fori(lo // 2, hi // 2) as i:
        for v in range(2):
            for lag, stage in stages:
                stage(i * 2 + (v - lag), (v - lag) % 2, i + (v - lag) // 2)
    straight(range(hi, n + deepest))


def build(nc, x, a, b, w_out, b_out, router_w, w1, w2, out, xh_rows, xs_rows, y_rows):
    B, S, D = x.shape
    E, _, H = w1.shape
    N = B * S
    NT = N // P
    DC = D // P
    HC = H // P
    K = 2
    CT = 2
    CH = CT * P
    NCH = N // CH
    NJ = (K * N - E) // P + E
    WE = DC * H
    assert S == 2 * CH and WE == HC * D and DC == 2 and NT * E <= 512

    x_c = x.rearrange("b (h k p) d -> (b h) p k d", h=2, p=P)
    out_c = out.rearrange("b (h k p) d -> (b h) p k d", h=2, p=P)
    xh_c = xh_rows.rearrange("(c k p) n -> c p k n", k=CT, p=P)
    xs_c = xs_rows.rearrange("(c k p) n -> c p k n", k=CT, p=P)
    y_c = y_rows.rearrange("(s c k p) n -> s c p k n", s=K, k=CT, p=P)
    w_c = [w1.rearrange("e (c p) h -> e p c h", p=P), w2.rearrange("e (c p) n -> e p c n", p=P)]

    with ExitStack() as ctx:
        def sb(name, shape, dt):
            return ctx.enter_context(nc.sbuf_tensor(name, shape, dt))

        def sem(name):
            return ctx.enter_context(nc.semaphore(name))

        def pair(name):
            return [sem(f"{name}{u}") for u in range(2)]

        bank = [ctx.enter_context(nc.psum_tensor(f"bank{i}", [P, 512], F32)) for i in range(8)]

        wbuf = [sb(f"wbuf{m}", [P, E + 1, WE], F32) for m in range(2)]
        spare = [w[:, 0, :] for w in wbuf]
        wpart = [w[:, :, :].rearrange("p e n -> p (e n)").bitcast(F16) for w in wbuf]

        def w16(m, e, off, n):
            return wpart[m][:, bass.ds(e * (2 * WE) + off, n)]

        ident = sb("ident", [P, P], F32)
        ident16 = sb("ident16", [P, P], F16)
        before16 = sb("before16", [P, P], F16)
        ones16 = sb("ones16", [P, P], F16)
        rev = sb("rev", [P, NT, E], F32)
        iota_r = sb("iota_r", [P, P], F32)
        keep = sb("keep", [P, E, NT], F32)
        tile_k = sb("tile_k", [P, E, NT], F32)
        code = sb("code", [P, NT], F32)
        iota_j = sb("iota_j", [P, NJ, E], F32)
        zero_e = sb("zero_e", [P, E], F32)
        one_e = sb("one_e", [P, E], F32)

        ab = sb("ab", [P, 2, DC], F32)
        th = sb("th", [P, DC], F32)
        decay = spare[1][:, 0:512].rearrange("p (c n) -> p c n", c=DC)
        bout = spare[1][:, 512:1024].rearrange("p (c n) -> p c n", c=CT)
        woT = spare[1][:, 1024:1536].rearrange("p (c n) -> p c n", c=DC)
        wo = spare[0][:, 0:512].rearrange("p (c n) -> p c n", c=DC)
        rw = spare[0][0:E, 512:512 + D]
        ones_ch = spare[0][:, 768:768 + CH]
        rwT = sb("rwT", [P, DC, E], F32)

        def ring(name, shape, dt):
            return [sb(f"{name}{u}", shape, dt) for u in range(2)]

        xin = ring("xin", [P, CT, D], F32)
        xpb = ring("xpb", [P, CT, D], F32)
        ybx = ring("ybx", [P, 2, DC, CH], F32)
        y = [v[:, 0] for v in ybx]
        bx = [v[:, 1] for v in ybx]
        res = ring("res", [P, CT, D], F32)
        xs = ring("xs", [P, CT, D], F32)
        xhl = ring("xhl", [P, CT, 2 * D], F16)
        xsT = ring("xsT", [P, DC * CH], F32)
        stats = ring("stats", [P, CT, 6], F32)
        mv = ring("mv", [P, CT, 2], F32)
        std = ring("std", [P, CT], F32)
        rstd = ring("rstd", [P, CT], F32)
        shift = ring("shift", [P, CT], F32)
        eps1 = sb("eps1", [P, 1], F32)
        eps2 = sb("eps2", [P, 1], F32)

        junk = spare[0][:, 1024:2048].bitcast(BF16)
        sq = sb("sq", [P, 2, E], F32)
        sqm = sb("sqm", [P, 2], F32)
        sqa = sb("sqa", [P, 2], F32)
        top = sb("top", [P, 2], F32)
        pow2 = sb("pow2", [P, 2], F32)
        ipow2 = sb("ipow2", [P, 2], F32)
        ws = sb("ws", [P, 2], F32)
        hs = sb("hs", [P, 1], F32)
        unz = sb("unz", [P, 1], F32)
        uny = sb("uny", [P, 1], F32)

        def rt(name, shape=(P, NT, E), dt=F32):
            return sb(name, list(shape), dt)

        lg, ex, pr = rt("lg"), rt("ex"), rt("pr")
        eq, oh1, oh2 = rt("eq"), rt("oh1"), rt("oh2")
        mx, sm, rs = rt("mx", (P, NT)), rt("sm", (P, NT)), rt("rs", (P, NT))
        p1, p2, k1 = rt("p1", (P, NT)), rt("p2", (P, NT)), rt("k1", (P, NT))
        wab = rt("wab", (P, K, NT))
        both = rt("both", (P, E, NT), F16)
        ptot, incl, slot = rt("ptot", (P, E, NT)), rt("incl", (P, E, NT)), rt("slot", (P, E, NT))
        cnt, nt, endt, base = rt("cnt", (P, E)), rt("nt", (P, E)), rt("endt", (P, E)), rt("base", (P, E))
        sl = rt("sl", (P, K, NT))
        sli, slr_i, slj_i = (rt(n, (P, K, NT), I32) for n in ("sli", "slr_i", "slj_i"))
        slr, slj = rt("slr", (P, K, NT)), rt("slj", (P, K, NT))
        past = rt("past", (1, NJ, E))
        expf = rt("expf", (1, NJ))
        expert = rt("expert", (1, NJ + 1), I32)
        row1h = [rt(f"row1h{i}", (P, P), F16) for i in range(4)]
        col1h = [rt(f"col1h{i}", (P, NJ), F16) for i in range(4)]
        v0, vs, va, vneg, vk = (rt(n, (P, NJ)) for n in ("v0", "vs", "va", "vneg", "vk"))
        tok = rt("tok", (P, NJ))
        src = rt("src", (P, NJ), U32)
        dst = rt("dst", (P, NJ), U32)

        isrc = ring("isrc", [P, 1], U32)
        idst = ring("idst", [P, 1], U32)
        xg = [v[:, 0] for v in xhl]
        xgT = [v[:, 1] for v in xhl]
        g = [v[:, :, :, :].rearrange("p s c n -> p (s c n)") for v in ybx]
        hh = [v[:, :].bitcast(F16) for v in xsT]
        hl = [v[:, :, :].rearrange("p k d -> p (k d)").bitcast(F16) for v in xpb]
        ys = [v[:, 0] for v in res]

        xf, yf0, yf1, rf, of = bx, xpb, xin, res, xs
        yf = [yf0, yf1]

        small_loaded = sem("small_loaded")
        consts_made = sem("consts_made")
        iota_made = sem("iota_made")
        th_ready = sem("th_ready")
        decay_ready = sem("decay_ready")
        param_T = sem("param_T")
        param_ready = sem("param_ready")
        x_loaded = pair("x_loaded")
        xT_done = sem("xT_done")
        bx_done = sem("bx_done")
        scan_done = sem("scan_done")
        proj_done = sem("proj_done")
        xpb_done = sem("xpb_done")
        add_done = sem("add_done")
        stat_done = sem("stat_done")
        mv_done = sem("mv_done")
        std_done = sem("std_done")
        rstd_done = sem("rstd_done")
        norm_done = sem("norm_done")
        hi_done = sem("hi_done")
        lo_done = sem("lo_done")
        xh_stored = pair("xh_stored")
        xs_stored = pair("xs_stored")
        t2_done = sem("t2_done")
        xsT_done = sem("xsT_done")
        logit_done = sem("logit_done")
        w_loaded = pair("w_loaded")
        sq_done = sem("sq_done")
        sqa_done = sem("sqa_done")
        top_done = sem("top_done")
        scales_ready = sem("scales_ready")
        whi_done = sem("whi_done")
        w_ready = sem("w_ready")
        dve_step = sem("dve_step")
        ex_in = sem("ex_in")
        ex_out = sem("ex_out")
        both_ready = sem("both_ready")
        rank_done = sem("rank_done")
        onehot_ready = sem("onehot_ready")
        onehot_used = sem("onehot_used")
        place_done = sem("place_done")
        route_ready = sem("route_ready")
        isrc_ready = sem("isrc_ready")
        idst_ready = sem("idst_ready")
        xg_loaded = pair("xg_loaded")
        xgT_done = sem("xgT_done")
        xgT_ready = sem("xgT_ready")
        up_done = sem("up_done")
        gelu_done = sem("gelu_done")
        hh_done = sem("hh_done")
        h_ready = sem("h_ready")
        down_done = sem("down_done")
        ys_ready = sem("ys_ready")
        y_stored = pair("y_stored")
        f_loaded = pair("f_loaded")
        f_half = sem("f_half")
        f_sum = sem("f_sum")
        f_stat = sem("f_stat")
        f_mv = sem("f_mv")
        f_std = sem("f_std")
        f_rstd = sem("f_rstd")
        f_out = sem("f_out")
        f_stored = pair("f_stored")

        def apart(eng, semaphore, value):
            eng.wait_ge(semaphore, value)
            eng.sem_inc(passed, 1)

        passed = sem("passed")
        block = ctx.enter_context(nc.Block())

        @block.sync
        def _(sp):
            def load_x(c, u, half):
                if later(c):
                    sp.wait_ge(xT_done, c - 1)
                    sp.wait_ge(xpb_done, c - 1)
                sp.dma_start(xin[u][:, :, :], x_c[bass.ds(c, 1)].rearrange("a p k d -> (a p) k d")
                             ).then_inc(x_loaded[u], 16)

            def store_x(c, u, half):
                sp.wait_ge(norm_done, c + 1)
                sp.dma_start(xs_c[bass.ds(c, 1)].rearrange("a p k n -> (a p) k n"), xs[u][:, :, :]
                             ).then_inc(xs_stored[u], 16)
                sp.wait_ge(hi_done, c + 1)
                sp.wait_ge(lo_done, c + 1)
                sp.dma_start(xh_c[bass.ds(c, 1)].rearrange("a p k n -> (a p) k n"), xhl[u][:, :, :]
                             ).then_inc(xh_stored[u], 16)

            for c in range(2):
                load_x(c, c, 0)
            with nc.allow_non_contiguous_dma(reason="two vectors, one element a partition"):
                sp.dma_start(ab[:, 0, :], a.rearrange("(c p) -> p c", p=P)).then_inc(small_loaded, 16)
                sp.dma_start(ab[:, 1, :], b.rearrange("(c p) -> p c", p=P)).then_inc(small_loaded, 16)
            sp.dma_start(wo[:, :, :], w_out.rearrange("(c p) d -> p c d", p=P)).then_inc(small_loaded, 16)
            sp.dma_start(rw[:, :], router_w).then_inc(small_loaded, 16)
            for k in range(CT):
                sp.dma_start(bout[:, k, :], b_out.partition_broadcast(P)).then_inc(small_loaded, 16)
            skewed(sp, NCH - 2, [(0, lambda c, u, half: load_x(c + 2, u, half + 1)),
                                 (2, store_x)])
            for c in range(NCH - 2, NCH):
                store_x(c, c % 2, c // 2)

            def load_f(c, u, half):
                if later(c):
                    sp.wait_ge(f_sum, CT * (c - 1))
                sp.dma_start(xf[u][:, :, :], xs_c[bass.ds(c, 1)].rearrange("a p k n -> (a p) k n")
                             ).then_inc(f_loaded[u], 16)
                for s in range(K):
                    sp.dma_start(yf[s][u][:, :, :],
                                 y_c[s, bass.ds(c, 1)].rearrange("a p k n -> (a p) k n")
                                 ).then_inc(f_loaded[u], 16)

            def store_f(c, u, half):
                sp.wait_ge(f_out, CT * (c + 1))
                sp.dma_start(out_c[bass.ds(c, 1)].rearrange("a p k d -> (a p) k d"), of[u][:, :, :]
                             ).then_inc(f_stored[u], 16)

            for u in range(2):
                sp.wait_ge(xs_stored[u], 16 * (NCH // 2))
                sp.wait_ge(y_stored[u], 16 * ((NJ + 1 - u) // 2))
            skewed(sp, NCH, [(0, load_f), (2, store_f)])
            for u in range(2):
                sp.wait_ge(f_stored[u], 16 * (NCH // 2))

        @block.gpsimd
        def _(pool):
            made = [0]

            def fill(ins):
                made[0] += 1
                ins.then_inc(iota_made, 1)
                pool.wait_ge(iota_made, made[0])

            nc.gpsimd.memset(ones_ch[:, :], 1.0)
            nc.gpsimd.memset(eps1[:, :], EPS / XS ** 2)
            nc.gpsimd.memset(eps2[:, :], EPS * XS ** 2)
            fill(nc.gpsimd.memset(ident[:, :], 0.0))
            fill(nc.gpsimd.affine_select(out=ident[:, :], in_=ident[:, :], compare_op=ALU.not_equal, fill=1.0,
                                         base=0, pattern=[[-1, P]], channel_multiplier=1))
            nc.gpsimd.tensor_copy(ident16[:, :], ident[:, :]).then_inc(consts_made, 1)

            def residual(c, u, half):
                pool.wait_ge(x_loaded[u], 16 * (half + 1))
                if later(c):
                    pool.wait_ge(add_done, c - 1)
                nc.gpsimd.tensor_tensor(xpb[u][:, :, :], xin[u][:, :, :], bout[:, :, :], ALU.add
                                        ).then_inc(xpb_done, 1)

            def low_part(c, u, half):
                pool.wait_ge(hi_done, c + 1)
                nc.gpsimd.tensor_tensor(xhl[u][:, :, D:2 * D], xs[u][:, :, :], xhl[u][:, :, 0:D], ALU.subtract
                                        ).then_inc(lo_done, 1)

            pool.wait_ge(small_loaded, 16 * 6)
            skewed(pool, NCH, [(0, residual), (3, low_part)])

            fill(nc.gpsimd.memset(ones16[:, :], 1.0))
            nc.gpsimd.affine_select(out=before16[:, :], in_=ones16[:, :], compare_op=ALU.is_gt, fill=0.0,
                                    base=0, pattern=[[1, P]], channel_multiplier=-1)
            nc.gpsimd.iota(rev[:, :, :], pattern=[[0, NT], [-1, E]], base=E, channel_multiplier=0,
                           allow_small_or_imprecise_dtypes=True)
            nc.gpsimd.iota(iota_r[:, :], pattern=[[1, P]], base=0, channel_multiplier=0,
                           allow_small_or_imprecise_dtypes=True)
            nc.gpsimd.iota(tile_k[:, :, :], pattern=[[0, E], [P, NT]], base=0, channel_multiplier=0,
                           allow_small_or_imprecise_dtypes=True)
            nc.gpsimd.iota(iota_j[:, :, :], pattern=[[1, NJ], [0, E]], base=0, channel_multiplier=0,
                           allow_small_or_imprecise_dtypes=True)
            nc.gpsimd.iota(code[:, 0:NT // 2], pattern=[[P, NT // 2]], base=1, channel_multiplier=1,
                           allow_small_or_imprecise_dtypes=True)
            nc.gpsimd.iota(code[:, NT // 2:NT], pattern=[[-P, NT // 2]], base=-1, channel_multiplier=-1,
                           allow_small_or_imprecise_dtypes=True)
            nc.gpsimd.memset(keep[:, :, 1:NT], 1.0)
            nc.gpsimd.memset(keep[:, :, 0:1], 0.0)
            nc.gpsimd.memset(one_e[:, :], 1.0)
            nc.gpsimd.memset(zero_e[:, :], 0.0).then_inc(consts_made, 1)

            pool.wait_ge(sqa_done, 1)
            nc.gpsimd.partition_all_reduce(sqa[:, :], sqm[:, :], P, bass.bass_isa.ReduceOp.max
                                           ).then_inc(sqa_done, 1)

            def gather(j, u, half):
                if later(j):
                    apart(pool, xg_loaded[u], 16 * half)
                nc.gpsimd.tensor_copy(isrc[u][:, :], src[:, bass.ds(j, 1)]).then_inc(isrc_ready, 1)
                pool.wait_ge(isrc_ready, j + 1)
                if later(j):
                    apart(pool, xgT_done, j - 1)
                nc.gpsimd.indirect_dma_start(
                    out=xg[u][:, :], out_offset=None, in_=xh_rows,
                    in_offset=bass.IndirectOffsetOnAxis(ap=isrc[u][:, 0:1], axis=0)).then_inc(xg_loaded[u], 16)

            def scatter(j, u, half):
                if later(j):
                    apart(pool, y_stored[u], 16 * half)
                nc.gpsimd.tensor_copy(idst[u][:, :], dst[:, bass.ds(j, 1)]).then_inc(idst_ready, 1)
                pool.wait_ge(idst_ready, j + 1)
                apart(pool, ys_ready, j + 1)
                nc.gpsimd.indirect_dma_start(
                    out=y_rows, out_offset=bass.IndirectOffsetOnAxis(ap=idst[u][:, 0:1], axis=0),
                    in_=ys[u][:, :], in_offset=None, bounds_check=K * N - 1, oob_is_err=False
                    ).then_inc(y_stored[u], 16)

            for u in range(2):
                pool.wait_ge(xh_stored[u], 16 * (NCH // 2))
            pool.wait_ge(route_ready, 1)
            skewed(pool, NJ, [(0, gather), (3, scatter)])

        @block.tensor
        def _(pe):
            def transpose_x(c, u, half):
                pe.wait_ge(x_loaded[u], 16 * (half + 1))
                if later(c):
                    pe.wait_ge(bx_done, c - 1)
                for dc in range(DC):
                    for k in range(CT):
                        last = pe.transpose(bank[u][:, dc * CH + k * P:dc * CH + (k + 1) * P],
                                            xin[u][:, k, dc * P:(dc + 1) * P], ident[:, :])
                last.then_inc(xT_done, 1)

            def project(c, u, half):
                pe.wait_ge(scan_done, c + 1)
                if later(c):
                    pe.wait_ge(add_done, c - 1)
                for k in range(CT):
                    for dc in range(DC):
                        last = pe.matmul(bank[2 + u][:, k * D:(k + 1) * D], y[u][:, dc, k * P:(k + 1) * P],
                                         woT[:, dc, :], start=(dc == 0), stop=(dc == DC - 1))
                last.then_inc(proj_done, 1)

            def transpose_xs(c, u, half):
                pe.wait_ge(norm_done, c + 1)
                if later(c):
                    pe.wait_ge(xsT_done, c - 1)
                for dc in range(DC):
                    for k in range(CT):
                        last = pe.transpose(bank[4 + u][:, dc * CH + k * P:dc * CH + (k + 1) * P],
                                            xs[u][:, k, dc * P:(dc + 1) * P], ident[:, :])
                last.then_inc(t2_done, 1)

            def logits(c, u, half):
                pe.wait_ge(xsT_done, c + 1)
                for k in range(CT):
                    for dc in range(DC):
                        last = pe.matmul(bank[6][:, bass.ds((c * CT + k) * E, E)],
                                         xsT[u][:, dc * CH + k * P:dc * CH + (k + 1) * P],
                                         rwT[:, dc, :], start=(dc == 0), stop=(dc == DC - 1))
                last.then_inc(logit_done, 1)

            pe.wait_ge(consts_made, 1)
            pe.wait_ge(small_loaded, 16 * 6)
            for dc in range(DC):
                for ec in range(DC):
                    pe.transpose(bank[7][:, dc * D + ec * P:dc * D + (ec + 1) * P],
                                 wo[:, ec, dc * P:(dc + 1) * P], ident[:, :])
                last = pe.transpose(bank[6][:, dc * E:(dc + 1) * E], rw[:, dc * P:(dc + 1) * P],
                                    ident[0:E, 0:E])
            last.then_inc(param_T, 1)
            pe.wait_ge(param_ready, 1)
            skewed(pe, NCH, [(0, transpose_x), (2, project), (4, transpose_xs), (5, logits)])

            pe.wait_ge(both_ready, 1)
            pe.wait_ge(consts_made, 2)
            both_v = both[:, :, :].rearrange("p e t -> p (e t)")
            pe.matmul(bank[5][:, 0:E * NT], before16[:, :], both_v, start=True, stop=True)
            pe.matmul(bank[4][:, 0:E * NT], ones16[:, :], both_v, start=True, stop=True).then_inc(rank_done, 1)

            for t in range(NT):
                for k in range(K):
                    n = t * K + k
                    pe.wait_ge(onehot_ready, n + 1)
                    pe.matmul(bank[k][:, 0:NJ], row1h[n % 4][:, :], col1h[n % 4][:, :],
                              start=(t == 0), stop=(t == NT - 1)).then_inc(onehot_used, 1)

            def transpose_g(j, u, half):
                pe.wait_ge(xg_loaded[u], 16 * (half + 1))
                if later(j):
                    pe.wait_ge(xgT_ready, j - 1)
                t16 = bank[4 + u][:, :].bitcast(F16)
                for q in range(4):
                    last = pe.transpose(t16[:, q * P:(q + 1) * P], xg[u][:, q * P:(q + 1) * P], ident16[:, :])
                last.then_inc(xgT_done, 1)

            def up(j, u, half):
                pe.wait_ge(xgT_ready, j + 1)
                e = pe.value_load(expert[0:1, bass.ds(j, 1)], min_val=0, max_val=E - 1)
                if later(j):
                    pe.wait_ge(gelu_done, 2 * (j - 1))
                hi, lo = xgT[u][:, 0:D], xgT[u][:, D:2 * D]
                for hc in range(HC):
                    o = bank[2 * u + hc // 4][:, (hc % 4) * P:(hc % 4 + 1) * P]
                    for dc in range(DC):
                        c = slice(dc * P, (dc + 1) * P)
                        w_hi = w16(0, e, dc * H + hc * P, P)
                        w_lo = w16(0, e, WE + dc * H + hc * P, P)
                        pe.matmul(o, w_hi, hi[:, c], start=(dc == 0), stop=False)
                        pe.matmul(o, w_hi, lo[:, c], start=False, stop=False)
                        last = pe.matmul(o, w_lo, hi[:, c], start=False, stop=(dc == DC - 1))
                    if hc % 4 == 3:
                        last.then_inc(up_done, 1)

            def down(j, u, half):
                e = pe.value_load(expert[0:1, bass.ds(j, 1)], min_val=0, max_val=E - 1)
                if later(j):
                    pe.wait_ge(ys_ready, j - 1)
                o = bank[6 + u][:, 0:D]
                for hc in range(HC):
                    if hc % 4 == 0:
                        pe.wait_ge(h_ready, 2 * j + hc // 4 + 1)
                    c = slice(hc * P, (hc + 1) * P)
                    w_hi = w16(1, e, hc * D, D)
                    w_lo = w16(1, e, WE + hc * D, D)
                    pe.matmul(o, hh[u][:, c], w_hi, start=(hc == 0), stop=False)
                    pe.matmul(o, hh[u][:, c], w_lo, start=False, stop=False)
                    last = pe.matmul(o, hl[u][:, c], w_hi, start=False, stop=(hc == HC - 1))
                last.then_inc(down_done, 1)

            pe.wait_ge(route_ready, 1)
            pe.wait_ge(w_ready, 2 * E)
            skewed(pe, NJ, [(0, transpose_g), (1, up), (2, down)])

        @block.scalar
        def _(act):
            def load_w(n):
                act.dma_start(wbuf[n % 2][:, bass.ds(n // 2 + 1, 1), :].rearrange("p a n -> p (a n)"),
                              w_c[n % 2][n // 2]).then_inc(w_loaded[n % 2], 16)

            def square_w(c, u, half):
                act.wait_ge(w_loaded[u], 16 * (half + 1))
                act.wait_ge(sq_done, c)
                act.activation(junk[:, :], wbuf[u][:, bass.ds(half + 1, 1), :].rearrange("p a n -> p (a n)"),
                               ACT.Square, accum_out=sq[:, u, bass.ds(half, 1)]).then_inc(sq_done, 1)

            def load_weights(c, u, half):
                dstv = wbuf[u][:, bass.ds(half + 1, 1), :].rearrange("p a (c n) -> p (a c) n", c=w_c[u].shape[2])
                act.dma_start(dstv, w_c[u][bass.ds(half, 1)].rearrange("a p c n -> (a p) c n")
                              ).then_inc(w_loaded[u], 16)

            def scale_b(c, u, half):
                act.wait_ge(xT_done, c + 1)
                if later(c):
                    act.wait_ge(scan_done, c - 1)
                for dc in range(DC):
                    last = act.activation(bx[u][:, dc, :], bank[u][:, dc * CH:(dc + 1) * CH], ACT.Copy,
                                          scale=ab[:, 1, dc:dc + 1])
                last.then_inc(bx_done, 1)

            def deviation(c, u, half):
                act.wait_ge(mv_done, c + 1)
                if later(c):
                    act.wait_ge(rstd_done, c - 1)
                act.activation(std[u][:, :], mv[u][:, :, 1], ACT.Sqrt, bias=eps1[:, 0:1], scale=XS ** -2
                               ).then_inc(std_done, 1)

            def high_part(c, u, half):
                act.wait_ge(norm_done, c + 1)
                if later(c):
                    act.wait_ge(xh_stored[u], 16 * half)
                    act.wait_ge(lo_done, c - 1)
                act.activation(xhl[u][:, :, 0:D], xs[u][:, :, :], ACT.Copy).then_inc(hi_done, 1)

            def copy_xsT(c, u, half):
                act.wait_ge(t2_done, c + 1)
                if later(c):
                    act.wait_ge(logit_done, c - 1)
                act.activation(xsT[u][:, :], bank[4 + u][:, :], ACT.Copy).then_inc(xsT_done, 1)

            act.wait_ge(small_loaded, 16 * 6)
            act.activation(th[:, :], ab[:, 0, :], ACT.Tanh).then_inc(th_ready, 1)
            act.wait_ge(param_T, 1)
            act.activation(rwT[:, :, :].rearrange("p c e -> p (c e)"), bank[6][:, 0:DC * E], ACT.Copy)
            act.activation(woT[:, :, :].rearrange("p c e -> p (c e)"), bank[7][:, :], ACT.Copy
                           ).then_inc(param_ready, 1)
            act.wait_ge(consts_made, 1)
            skewed(act, NCH, [(0, scale_b), (3, deviation), (4, high_part), (4, copy_xsT),
                              (2, square_w), (0, load_weights)])

            act.wait_ge(sqa_done, 2)
            act.activation(top[:, :], sqa[:, :], ACT.Sqrt).then_inc(top_done, 1)
            act.wait_ge(ex_in, 1)
            act.activation(ex[:, :, :], ex[:, :, :], ACT.Exp, scale=1.0 / XS).then_inc(ex_out, 1)

            act.wait_ge(scales_ready, 1)
            for e in range(E):
                for m in range(2):
                    n = 2 * e + m
                    if e:
                        act.wait_ge(w_ready, n - 1)
                    act.activation(w16(m, e, 0, WE), wbuf[m][:, e + 1, :], ACT.Copy, scale=ws[:, m:m + 1]
                                   ).then_inc(whi_done, 1)

            def gelu(j, u, half):
                for q in range(2):
                    act.wait_ge(up_done, 2 * j + q + 1)
                    if later(j):
                        act.wait_ge(h_ready, 2 * (j - 1))
                    act.activation(g[u][:, q * 512:(q + 1) * 512], bank[2 * u + q][:, :], ACT.Gelu,
                                   scale=unz[:, 0:1]).then_inc(gelu_done, 1)

            def copy_y(j, u, half):
                act.wait_ge(down_done, j + 1)
                if later(j):
                    act.wait_ge(y_stored[u], 16 * half)
                act.activation(ys[u][:, :], bank[6 + u][:, 0:D], ACT.Copy).then_inc(ys_ready, 1)

            skewed(act, NJ, [(0, gelu), (1, copy_y)])

            def f_deviation(c, u, half):
                act.wait_ge(f_mv, c + 1)
                if later(c):
                    act.wait_ge(f_rstd, 2 * (c - 1))
                act.activation(std[u][:, :], mv[u][:, :, 1], ACT.Sqrt, bias=eps2[:, 0:1]).then_inc(f_std, 1)

            def f_apply(c, u, half):
                act.wait_ge(f_rstd, 2 * (c + 1))
                if later(c):
                    act.wait_ge(f_stored[u], 16 * half)
                for k in range(CT):
                    act.activation(of[u][:, k, :], rf[u][:, k, :], ACT.Identity, bias=shift[u][:, k:k + 1],
                                   scale=rstd[u][:, k:k + 1]).then_inc(f_out, 1)

            skewed(act, NCH, [(0, f_deviation), (1, f_apply)])

        @block.vector
        def _(dve):
            def scan(c, u, half):
                dve.wait_ge(bx_done, c + 1)
                if later(c):
                    dve.wait_ge(proj_done, c - 1)
                if u == 1:
                    dve.wait_ge(scan_done, c)
                for dc in range(DC):
                    last = dve.tensor_tensor_scan(
                        out=y[u][:, dc, :], data0=decay[:, dc, :], data1=bx[u][:, dc, :],
                        initial=0.0 if u == 0 else y[0][:, dc, CH - 1:CH], op0=ALU.mult, op1=ALU.add)
                last.then_inc(scan_done, 1)

            def add(c, u, half):
                dve.wait_ge(proj_done, c + 1)
                dve.wait_ge(xpb_done, c + 1)
                dve.tensor_tensor(res[u][:, :, :].rearrange("p k d -> p (k d)"), bank[2 + u][:, :],
                                  xpb[u][:, :, :].rearrange("p k d -> p (k d)"), ALU.add).then_inc(add_done, 1)

            def statistics(c, u, half):
                dve.wait_ge(add_done, c + 1)
                for k in range(CT):
                    last = dve.bn_stats(stats[u][:, k, :], res[u][:, k, :])
                last.then_inc(stat_done, 1)
                apart(dve, stat_done, c + 1)
                for k in range(CT):
                    last = dve.bn_aggr(mv[u][:, k, :], stats[u][:, k, :])
                last.then_inc(mv_done, 1)

            def normalise(c, u, half):
                dve.wait_ge(std_done, c + 1)
                dve.reciprocal(rstd[u][:, :], std[u][:, :]).then_inc(rstd_done, 1)
                if later(c):
                    dve.wait_ge(xs_stored[u], 16 * half)
                    dve.wait_ge(t2_done, c - 1)
                    dve.wait_ge(hi_done, c - 1)
                    dve.wait_ge(lo_done, c - 1)
                dve.wait_ge(rstd_done, c + 1)
                for k in range(CT):
                    last = dve.tensor_scalar(xs[u][:, k, :], res[u][:, k, :], mv[u][:, k, 0:1],
                                             rstd[u][:, k:k + 1], ALU.subtract, ALU.mult)
                last.then_inc(norm_done, 1)

            dve.wait_ge(th_ready, 1)
            dve.wait_ge(consts_made, 1)
            for dc in range(DC):
                last = dve.tensor_scalar(decay[:, dc, :], ones_ch[:, :], th[:, dc:dc + 1], None, ALU.mult)
            last.then_inc(decay_ready, 1)
            dve.wait_ge(decay_ready, 1)
            skewed(dve, NCH, [(1, scan), (2, add), (3, normalise), (2, statistics)])

            step = [0]

            def link(ins):
                step[0] += 1
                ins.then_inc(dve_step, 1)
                dve.wait_ge(dve_step, step[0])

            def over_e(v):
                return v[:, :].unsqueeze(2).to_broadcast([P, NT, E])

            def over_t(v):
                return v[:, :].unsqueeze(2).to_broadcast([P, E, NT])

            def te(v):
                return v[:, :, :].rearrange("p e t -> p t e")

            dve.wait_ge(sq_done, 2 * E)
            dve.tensor_reduce(sqm[:, :], sq[:, :, :], AX.X, ALU.max).then_inc(sqa_done, 1)

            dve.wait_ge(logit_done, NCH)
            dve.wait_ge(consts_made, 2)
            link(dve.tensor_copy(lg[:, :, :].rearrange("p t e -> p (t e)"), bank[6][:, 0:NT * E]))
            link(dve.tensor_reduce(mx[:, :], lg[:, :, :], AX.X, ALU.max))
            dve.tensor_tensor(ex[:, :, :], lg[:, :, :], over_e(mx), ALU.subtract).then_inc(ex_in, 1)

            dve.wait_ge(top_done, 1)
            link(dve.tensor_scalar(top[:, :], top[:, :], 2.0 ** -40, None, ALU.max))
            link(dve.tensor_scalar(pow2[:, :].bitcast(I32), top[:, :].bitcast(I32), 0x7F800000, None,
                                   ALU.bitwise_and))
            link(dve.reciprocal(ipow2[:, :], pow2[:, :]))
            link(dve.tensor_scalar(ws[:, :], ipow2[:, :], S_TOP, None, ALU.mult))
            dve.tensor_scalar(unz[:, :], pow2[:, 0:1], 1.0 / (S_TOP * XS), None, ALU.mult)
            link(dve.tensor_scalar(hs[:, :], ipow2[:, 0:1], S_TOP / 256, None, ALU.mult))
            dve.scalar_tensor_tensor(out=uny[:, :], in0=pow2[:, 0:1], scalar=256 * XS / S_TOP ** 2,
                                     in1=pow2[:, 1:2], op0=ALU.mult, op1=ALU.mult).then_inc(scales_ready, 1)

            dve.wait_ge(ex_out, 1)
            link(dve.tensor_reduce(sm[:, :], ex[:, :, :], AX.X, ALU.add))
            link(dve.reciprocal(rs[:, :], sm[:, :]))
            link(dve.tensor_tensor(pr[:, :, :], ex[:, :, :], over_e(rs), ALU.mult))
            link(dve.tensor_reduce(p1[:, :], pr[:, :, :], AX.X, ALU.max))
            link(dve.tensor_tensor(eq[:, :, :], pr[:, :, :], over_e(p1), ALU.is_equal))
            link(dve.tensor_tensor(eq[:, :, :], eq[:, :, :], rev[:, :, :], ALU.mult))
            link(dve.tensor_reduce(k1[:, :], eq[:, :, :], AX.X, ALU.max))
            link(dve.tensor_tensor(oh1[:, :, :], rev[:, :, :], over_e(k1), ALU.is_equal))
            link(dve.scalar_tensor_tensor(out=pr[:, :, :], in0=oh1[:, :, :], scalar=-4.0, in1=pr[:, :, :],
                                          op0=ALU.mult, op1=ALU.add))
            link(dve.tensor_reduce(p2[:, :], pr[:, :, :], AX.X, ALU.max))
            link(dve.tensor_tensor(eq[:, :, :], pr[:, :, :], over_e(p2), ALU.is_equal))
            link(dve.tensor_tensor(eq[:, :, :], eq[:, :, :], rev[:, :, :], ALU.mult))
            link(dve.tensor_reduce(k1[:, :], eq[:, :, :], AX.X, ALU.max))
            link(dve.tensor_tensor(oh2[:, :, :], rev[:, :, :], over_e(k1), ALU.is_equal))
            dve.tensor_tensor(te(both), oh1[:, :, :], oh2[:, :, :], ALU.add).then_inc(both_ready, 1)
            link(dve.tensor_tensor(sm[:, :], p1[:, :], p2[:, :], ALU.add))
            link(dve.reciprocal(rs[:, :], sm[:, :]))
            link(dve.tensor_scalar(rs[:, :], rs[:, :], uny[:, 0:1], None, ALU.mult))
            dve.tensor_tensor(wab[:, 0, :], p1[:, :], rs[:, :], ALU.mult)
            dve.tensor_tensor(wab[:, 1, :], p2[:, :], rs[:, :], ALU.mult)

            dve.wait_ge(rank_done, 1)
            link(dve.tensor_copy(ptot[:, :, :].rearrange("p e t -> p (e t)"), bank[4][:, 0:E * NT]))
            link(dve.tensor_tensor_scan(out=incl[:, :, :].rearrange("p e t -> p (e t)"),
                                        data0=keep[:, :, :].rearrange("p e t -> p (e t)"),
                                        data1=ptot[:, :, :].rearrange("p e t -> p (e t)"),
                                        initial=0.0, op0=ALU.mult, op1=ALU.add))
            link(dve.tensor_copy(cnt[:, :], incl[:, :, NT - 1]))
            link(dve.tensor_tensor(slot[:, :, :], tile_k[:, :, :], over_t(cnt), ALU.is_lt))
            link(dve.tensor_reduce(nt[:, :], slot[:, :, :], AX.X, ALU.add))
            link(dve.tensor_tensor_scan(out=endt[:, :], data0=one_e[:, :], data1=nt[:, :], initial=0.0,
                                        op0=ALU.mult, op1=ALU.add))
            link(dve.tensor_tensor(base[:, :], endt[:, :], nt[:, :], ALU.subtract))
            link(dve.tensor_scalar(base[:, :], base[:, :], float(P), None, ALU.mult))
            link(dve.tensor_tensor(incl[:, :, :], incl[:, :, :], ptot[:, :, :], ALU.subtract))
            link(dve.tensor_tensor(incl[:, :, :], incl[:, :, :], over_t(base), ALU.add))
            link(dve.tensor_tensor(slot[:, :, :].rearrange("p e t -> p (e t)"), bank[5][:, 0:E * NT],
                                   incl[:, :, :].rearrange("p e t -> p (e t)"), ALU.add))
            dve.tensor_tensor(eq[:, :, :], oh1[:, :, :], te(slot), ALU.mult)
            link(dve.tensor_tensor(ex[:, :, :], oh2[:, :, :], te(slot), ALU.mult))
            dve.tensor_reduce(sl[:, 0, :], eq[:, :, :], AX.X, ALU.add)
            link(dve.tensor_reduce(sl[:, 1, :], ex[:, :, :], AX.X, ALU.add))
            link(dve.tensor_copy(sli[:, :, :], sl[:, :, :]))
            dve.tensor_scalar(slr_i[:, :, :], sli[:, :, :], P - 1, None, ALU.bitwise_and)
            link(dve.tensor_scalar(slj_i[:, :, :], sli[:, :, :], 7, None, ALU.logical_shift_right))
            dve.tensor_copy(slr[:, :, :], slr_i[:, :, :])
            link(dve.tensor_copy(slj[:, :, :], slj_i[:, :, :]))

            for t in range(NT):
                for k in range(K):
                    n = t * K + k
                    if n >= 4:
                        dve.wait_ge(onehot_used, n - 3)
                    dve.tensor_scalar(row1h[n % 4][:, :], iota_r[:, :], slr[:, k, t:t + 1], None, ALU.is_equal)
                    dve.tensor_scalar(col1h[n % 4][:, :], iota_r[:, 0:NJ], slj[:, k, t:t + 1],
                                      code[:, t:t + 1], ALU.is_equal, ALU.mult).then_inc(onehot_ready, 1)

            link(dve.tensor_tensor(past[:, :, :], iota_j[0:1, :, :],
                                   endt[0:1, :].unsqueeze(1).to_broadcast([1, NJ, E]), ALU.is_ge))
            link(dve.tensor_reduce(expf[:, :], past[:, :, :], AX.X, ALU.add))
            dve.tensor_scalar(expert[:, 0:NJ], expf[:, :], float(E - 1), None, ALU.min)

            dve.wait_ge(onehot_used, NT * K)
            link(dve.tensor_copy(v0[:, :], bank[0][:, 0:NJ]))
            dve.tensor_tensor(vs[:, :], bank[1][:, 0:NJ], v0[:, :], ALU.add)
            link(dve.tensor_scalar(vk[:, :], bank[1][:, 0:NJ], 0.0, float(N), ALU.not_equal, ALU.mult))
            link(dve.tensor_scalar(vneg[:, :], vs[:, :], 0.0, float(N // 2), ALU.is_lt, ALU.mult))
            dve.tensor_scalar(v0[:, :], vs[:, :], 0.0, 4.0 * N, ALU.is_equal, ALU.mult)
            link(dve.scalar_tensor_tensor(out=va[:, :], in0=vs[:, :], scalar=-1.0, in1=vs[:, :],
                                          op0=ALU.mult, op1=ALU.max))
            link(dve.tensor_tensor(va[:, :], va[:, :], vneg[:, :], ALU.add))
            link(dve.tensor_scalar(tok[:, :], va[:, :], -1.0, 0.0, ALU.add, ALU.max))
            dve.tensor_copy(src[:, :], tok[:, :])
            link(dve.tensor_tensor(tok[:, :], tok[:, :], vk[:, :], ALU.add))
            link(dve.tensor_tensor(tok[:, :], tok[:, :], v0[:, :], ALU.add))
            dve.tensor_copy(dst[:, :], tok[:, :]).then_inc(route_ready, 1)

            for e in range(E):
                for m in range(2):
                    dve.wait_ge(whi_done, 2 * e + m + 1)
                    dve.scalar_tensor_tensor(out=w16(m, e, WE, WE), in0=wbuf[m][:, e + 1, :],
                                             scalar=ws[:, m:m + 1], in1=w16(m, e, 0, WE),
                                             op0=ALU.mult, op1=ALU.subtract).then_inc(w_ready, 1)

            def columns(j, u, half):
                dve.wait_ge(xgT_done, j + 1)
                if later(j):
                    dve.wait_ge(up_done, 2 * (j - 1))
                dve.tensor_copy(xgT[u][:, :], bank[4 + u][:, :].bitcast(F16)[:, 0:2 * D]).then_inc(xgT_ready, 1)

            def split(j, u, half):
                if later(j):
                    dve.wait_ge(down_done, j - 1)
                for q in range(2):
                    c = slice(q * 512, (q + 1) * 512)
                    dve.wait_ge(gelu_done, 2 * j + q + 1)
                    dve.tensor_scalar(hh[u][:, c], g[u][:, c], hs[:, 0:1], None, ALU.mult).then_inc(hh_done, 1)
                    dve.wait_ge(hh_done, 2 * j + q + 1)
                    dve.scalar_tensor_tensor(out=hl[u][:, c], in0=g[u][:, c], scalar=hs[:, 0:1],
                                             in1=hh[u][:, c], op0=ALU.mult, op1=ALU.subtract
                                             ).then_inc(h_ready, 1)

            skewed(dve, NJ, [(0, columns), (1, split)])

            def f_first(c, u, half):
                dve.wait_ge(f_loaded[u], 48 * (half + 1))
                if later(c):
                    dve.wait_ge(f_out, CT * (c - 1))
                for s in range(K):
                    for k in range(CT):
                        last = dve.scalar_tensor_tensor(
                            out=rf[u][:, k, :], in0=yf[s][u][:, k, :], scalar=wab[:, s, bass.ds(c * CT + k, 1)],
                            in1=xf[u][:, k, :] if s == 0 else rf[u][:, k, :], op0=ALU.mult, op1=ALU.add)
                        last.then_inc(f_sum if s else f_half, 1)
                    if s == 0:
                        dve.wait_ge(f_half, CT * (c + 1))
                dve.wait_ge(f_sum, CT * (c + 1))
                for k in range(CT):
                    last = dve.bn_stats(stats[u][:, k, :], rf[u][:, k, :])
                last.then_inc(f_stat, 1)
                apart(dve, f_stat, c + 1)
                for k in range(CT):
                    last = dve.bn_aggr(mv[u][:, k, :], stats[u][:, k, :])
                last.then_inc(f_mv, 1)

            def f_second(c, u, half):
                dve.wait_ge(f_std, c + 1)
                if later(c):
                    dve.wait_ge(f_out, CT * (c - 1))
                dve.reciprocal(rstd[u][:, :], std[u][:, :]).then_inc(f_rstd, 1)
                dve.wait_ge(f_rstd, 2 * c + 1)
                dve.scalar_tensor_tensor(out=shift[u][:, :], in0=mv[u][:, :, 0], scalar=-1.0, in1=rstd[u][:, :],
                                         op0=ALU.mult, op1=ALU.mult).then_inc(f_rstd, 1)

            skewed(dve, NCH, [(0, f_first), (1, f_second)])


_INS = ["L0_attn_x", "L0_attn_a", "L0_attn_b", "L0_attn_w_out", "L0_attn_b_out", "L0_ffn_router_w", "L0_ffn_w1",
        "L0_ffn_w2"]


def kernel(**inputs):
    import numpy as np
    import concourse.bacc as bacc
    from concourse.bass_utils import run_bass_kernel_spmd

    nc = bacc.Bacc("TRN2", target_bir_lowering=False, num_devices=1)
    arrays, args = {}, []
    for name in _INS:
        v = np.ascontiguousarray(inputs[name])
        arrays[name] = v
        args.append(nc.dram_tensor(name, v.shape, mybir.dt.from_np(v.dtype), kind="ExternalInput").ap())
    B, S, D = inputs["L0_attn_x"].shape
    args.append(nc.dram_tensor("out", (B, S, D), F32, kind="ExternalOutput").ap())
    args.append(nc.dram_tensor("xh_rows", (B * S, 2 * D), F16, kind="Internal").ap())
    args.append(nc.dram_tensor("xs_rows", (B * S, D), F32, kind="Internal").ap())
    args.append(nc.dram_tensor("y_rows", (2 * B * S, D), F32, kind="Internal").ap())
    build(nc, *args)
    r = run_bass_kernel_spmd(nc, [arrays], core_ids=[0])
    return r.results[0]["out"]
```

```python
from contextlib import ExitStack

import concourse.bass as bass
from concourse import mybir

F32 = mybir.dt.float32
F16 = mybir.dt.float16
BF16 = mybir.dt.bfloat16
I32 = mybir.dt.int32
U32 = mybir.dt.uint32
ALU = mybir.AluOpType
ACT = mybir.ActivationFunctionType
AX = mybir.AxisListType

P = 128
EPS = 1e-5
XS = 2048.0
S_TOP = 16384.0


def later(c):
    return not isinstance(c, int) or c >= 2


def skewed(eng, n, stages, first=0):
    looped = [s for s in stages if s[0] is not None]
    deepest = max(lag for lag, _ in looped)
    lo = max(deepest + 2, first)
    lo += lo % 2
    hi = n - (n - lo) % 2

    def straight(steps):
        for s in steps:
            for lag, stage in stages:
                if lag is None:
                    if s < first:
                        stage(s)
                elif 0 <= s - lag < n:
                    stage(s - lag, (s - lag) % 2, (s - lag) // 2)

    straight(range(lo))
    with eng.Fori(lo // 2, hi // 2) as i:
        for v in range(2):
            for lag, stage in looped:
                stage(i * 2 + (v - lag), (v - lag) % 2, i + (v - lag) // 2)
    straight(range(hi, n + deepest))


def build(nc, x, a, b, w_out, b_out, router_w, w1, w2, out, xh_rows, xs_rows, w_rows):
    B, S, D = x.shape
    E, _, H = w1.shape
    N = B * S
    NT = N // P
    DC = D // P
    HC = H // P
    K = 2
    CT = 2
    CH = CT * P
    NCH = N // CH
    SUB = 2
    SL = SUB * P
    NJ = (K * N - E) // SL + E
    NQ = NJ * SUB
    FT = 4
    NF = NT // FT
    NH = NT // 2 * K
    WE = DC * H
    assert S == 2 * CH == FT * P and WE == HC * D and DC == 2 and NT * E <= 512

    x_c = x.rearrange("b (h k p) d -> (b h) p k d", h=2, p=P)
    out_f = out.rearrange("b (k p) d -> b p k d", p=P)
    xh_c = xh_rows.rearrange("(c k p) n -> c p k n", k=CT, p=P)
    xs_c = xs_rows[0:N, :].rearrange("(c k p) n -> c p k n", k=CT, p=P)
    xs_f = xs_rows[0:N, :].rearrange("(c k p) n -> c p k n", k=FT, p=P)
    w_c = [w1.rearrange("e (c p) h -> e p c h", p=P), w2.rearrange("e (c p) n -> e p c n", p=P)]

    with ExitStack() as ctx:
        def sb(name, shape, dt):
            return ctx.enter_context(nc.sbuf_tensor(name, shape, dt))

        def sem(name):
            return ctx.enter_context(nc.semaphore(name))

        def pair(name):
            return [sem(f"{name}{u}") for u in range(2)]

        bank = [ctx.enter_context(nc.psum_tensor(f"bank{i}", [P, 512], F32)) for i in range(8)]

        wbuf = [sb(f"wbuf{m}", [P, E + 1, WE], F32) for m in range(2)]
        spare = [w[:, 0, :] for w in wbuf]
        wpart = [w[:, :, :].rearrange("p e n -> p (e n)").bitcast(F16) for w in wbuf]

        def w16(m, e, off, n):
            return wpart[m][:, bass.ds(e * (2 * WE) + off, n)]

        ident = sb("ident", [P, P], F32)
        ident16 = sb("ident16", [P, P], F16)
        before16 = sb("before16", [P, P], F16)
        ones16 = sb("ones16", [P, P], F16)
        rev = sb("rev", [P, NT, E], F32)
        keep = sb("keep", [P, E, NT], F32)
        tile_k = sb("tile_k", [P, E, NT // 2], F32)
        code = sb("code", [P, 2, NH], F16)
        iota_j = sb("iota_j", [P, NJ, E], F32)
        dump = sb("dump", [P, NQ], F32)
        one_e = sb("one_e", [P, E], F32)

        ab = sb("ab", [P, 2, DC], F32)
        th = sb("th", [P, DC], F32)
        decay = spare[1][:, 0:512].rearrange("p (c n) -> p c n", c=DC)
        bout = spare[1][:, 512:1024].rearrange("p (c n) -> p c n", c=CT)
        woT = spare[1][:, 1024:1536].rearrange("p (c n) -> p c n", c=DC)
        wo = spare[0][:, 0:512].rearrange("p (c n) -> p c n", c=DC)
        rw = spare[0][0:E, 512:512 + D]
        ones_ch = spare[0][:, 768:768 + CH]
        rwT = sb("rwT", [P, DC, E], F32)

        arena = sb("arena", [P, 9216], F32)
        taken = [0]

        def part(shape, dt=F32):
            words = 1
            for d in shape:
                words *= d
            words = words * (1 if dt == F32 else 0.5)
            v = arena[:, int(taken[0]):int(taken[0] + words)]
            taken[0] += words
            assert taken[0] <= 9216
            v = v if dt == F32 else v.bitcast(dt)
            names = "abcd"[:len(shape)]
            return v.rearrange(f"p ({' '.join(names)}) -> p {' '.join(names)}", **dict(zip(names, shape)))

        def parts(shape, dt=F32):
            return [part(shape, dt) for _ in range(2)]

        def ring(name, shape, dt):
            return [sb(f"{name}{u}", shape, dt) for u in range(2)]

        xhl, xs = parts([CT, 2 * D], F16), parts([CT, D])
        xin, xpb, bx, y = parts([CT, D]), parts([CT, D]), parts([DC, CH]), parts([DC, CH])
        res, xsT = parts([CT, D]), parts([DC * CH])
        stats = ring("stats", [P, CT, 6], F32)
        mv = ring("mv", [P, CT, 2], F32)
        std = ring("std", [P, CT], F32)
        rstd = ring("rstd", [P, CT], F32)
        eps1 = sb("eps1", [P, 1], F32)
        eps2 = sb("eps2", [P, 1], F32)

        junk = spare[0][:, 1024:2048].bitcast(BF16)
        sq = sb("sq", [P, 2, E], F32)
        sqm = sb("sqm", [P, 2], F32)
        sqa = sb("sqa", [P, 2], F32)
        top = sb("top", [P, 2], F32)
        pow2 = sb("pow2", [P, 2], F32)
        ipow2 = sb("ipow2", [P, 2], F32)
        ws = sb("ws", [P, 2], F32)
        hs = sb("hs", [P, 1], F32)
        unz = sb("unz", [P, 1], F32)
        uny = sb("uny", [P, 1], F32)

        def rt(name, shape=(P, NT, E), dt=F32):
            return sb(name, list(shape), dt)

        ex, pr = rt("ex"), rt("pr")
        eq, oh1, oh2 = rt("eq"), rt("oh1"), rt("oh2")
        mx, sm, rs = rt("mx", (P, NT)), rt("sm", (P, NT)), rt("rs", (P, NT))
        p1, p2, k1 = rt("p1", (P, NT)), rt("p2", (P, NT)), rt("k1", (P, NT))
        wab = rt("wab", (P, K, NT))
        both = rt("both", (P, E, NT), F16)
        ptot, incl, slot = rt("ptot", (P, E, NT)), rt("incl", (P, E, NT)), rt("slot", (P, E, NT))
        cnt, nt, endt, base = rt("cnt", (P, E)), rt("nt", (P, E)), rt("endt", (P, E)), rt("base", (P, E))
        sl = rt("sl", (P, K, NT))
        sli, slr_i, slj_i = (rt(n, (P, K, NT), I32) for n in ("sli", "slr_i", "slj_i"))
        slr, slj = rt("slr", (P, NT * K), F16), rt("slj", (P, NT * K), F16)
        past = rt("past", (1, NJ, E))
        expf = rt("expf", (1, NJ))
        expert = rt("expert", (1, NJ + 1), I32)
        v0, vs, va, vneg, vk = (rt(n, (P, NQ)) for n in ("v0", "vs", "va", "vneg", "vk"))
        tok = rt("tok", (P, NQ))
        idx = rt("idx", (P, 3, NQ), U32)
        wabT = rt("wabT", (K * NT, P))
        taken[0] = 0
        iota_r = part([P, NH], F16)
        row1h = parts([P, NH], F16)
        col1h = parts([NQ, NH], F16)

        taken[0] = 0
        xg = parts([SUB, 2 * D], F16)
        xgT = parts([2 * DC, SL], F16)
        g = part([4, 512])
        hh = parts([HC, SL], F16)
        hl = parts([HC, SL], F16)
        ys = parts([SUB, D])
        ix = ring("ix", [P, SUB], U32)
        iw = ring("iw", [P, SUB], U32)
        iy = ring("iy", [P, SUB], U32)
        wsl = ring("wsl", [P, SUB], F32)

        rf = wbuf[0][:, :, :].rearrange("p e n -> p (e n)")[:, 0:NT * D].rearrange("p (t d) -> p t d", d=D)
        of = wbuf[1][:, :, :].rearrange("p e n -> p (e n)")[:, 0:NT * D].rearrange("p (t d) -> p t d", d=D)
        fstats = ring("fstats", [P, FT, 6], F32)
        fmv = ring("fmv", [P, FT, 2], F32)
        fstd = ring("fstd", [P, FT], F32)
        frstd = ring("frstd", [P, FT], F32)
        fshift = ring("fshift", [P, FT], F32)

        small_loaded = sem("small_loaded")
        consts_made = sem("consts_made")
        iota_made = sem("iota_made")
        th_ready = sem("th_ready")
        decay_ready = sem("decay_ready")
        param_T = sem("param_T")
        param_ready = sem("param_ready")
        x_loaded = pair("x_loaded")
        xT_done = sem("xT_done")
        bx_done = sem("bx_done")
        scan_done = sem("scan_done")
        proj_done = sem("proj_done")
        xpb_done = sem("xpb_done")
        add_done = sem("add_done")
        stat_done = sem("stat_done")
        mv_done = sem("mv_done")
        std_done = sem("std_done")
        rstd_done = sem("rstd_done")
        norm_done = sem("norm_done")
        hi_done = sem("hi_done")
        lo_done = sem("lo_done")
        xh_stored = pair("xh_stored")
        xs_stored = pair("xs_stored")
        t2_done = sem("t2_done")
        xsT_done = sem("xsT_done")
        logit_done = sem("logit_done")
        w_loaded = pair("w_loaded")
        sq_done = sem("sq_done")
        sqa_done = sem("sqa_done")
        top_done = sem("top_done")
        scales_ready = sem("scales_ready")
        whi_done = sem("whi_done")
        w_ready = sem("w_ready")
        dve_step = sem("dve_step")
        ex_in = sem("ex_in")
        ex_out = sem("ex_out")
        both_ready = sem("both_ready")
        rank_done = sem("rank_done")
        onehot_ready = sem("onehot_ready")
        onehot_used = sem("onehot_used")
        place_done = sem("place_done")
        route_ready = sem("route_ready")
        ix_ready = sem("ix_ready")
        iw_ready = sem("iw_ready")
        iy_ready = sem("iy_ready")
        wsl_loaded = pair("wsl_loaded")
        wabT_done = sem("wabT_done")
        wab_ready = sem("wab_ready")
        wabT_ready = sem("wabT_ready")
        w_stored = sem("w_stored")
        dump_ready = sem("dump_ready")
        xg_loaded = pair("xg_loaded")
        xgT_done = sem("xgT_done")
        xgT_ready = sem("xgT_ready")
        up_done = sem("up_done")
        gelu_done = sem("gelu_done")
        hh_done = sem("hh_done")
        h_ready = sem("h_ready")
        down_done = sem("down_done")
        ys_ready = sem("ys_ready")
        y_added = sem("y_added")
        f_loaded = pair("f_loaded")
        f_stat = sem("f_stat")
        f_mv = sem("f_mv")
        f_std = sem("f_std")
        f_rstd = sem("f_rstd")
        f_shift = sem("f_shift")
        f_out = sem("f_out")
        f_stored = pair("f_stored")

        def apart(eng, semaphore, value):
            eng.wait_ge(semaphore, value)
            eng.sem_inc(passed, 1)

        passed = sem("passed")
        block = ctx.enter_context(nc.Block())

        @block.sync
        def _(sp):
            def load_x(c, u, half):
                if later(c):
                    sp.wait_ge(xT_done, c - 1)
                    apart(sp, xpb_done, c - 1)
                sp.dma_start(xin[u], x_c[bass.ds(c, 1)].rearrange("a p k d -> (a p) k d")
                             ).then_inc(x_loaded[u], 16)

            def load_w(n, m, e):
                if later(n):
                    apart(sp, w_loaded[m], 16 * e)
                place = wbuf[m][:, bass.ds(e + 1, 1), :].rearrange("p a (c n) -> p (a c) n", c=w_c[m].shape[2])
                sp.dma_start(place, w_c[m][bass.ds(e, 1)].rearrange("a p c n -> (a p) c n")
                             ).then_inc(w_loaded[m], 16)

            load_x(0, 0, 0)
            with nc.allow_non_contiguous_dma(reason="two vectors, one element a partition"):
                sp.dma_start(ab[:, 0, :], a.rearrange("(c p) -> p c", p=P)).then_inc(small_loaded, 16)
                sp.dma_start(ab[:, 1, :], b.rearrange("(c p) -> p c", p=P)).then_inc(small_loaded, 16)
            sp.dma_start(wo, w_out.rearrange("(c p) d -> p c d", p=P)).then_inc(small_loaded, 16)
            sp.dma_start(rw, router_w).then_inc(small_loaded, 16)
            for k in range(CT):
                sp.dma_start(bout[:, k, :], b_out.partition_broadcast(P)).then_inc(small_loaded, 16)
            load_x(1, 1, 0)
            for c in range(2):
                load_w(c, c, 0)
            sp.wait_ge(small_loaded, 16 * 6)
            sp.dma_start(xs_rows[N:N + SL, :].rearrange("(k p) n -> p k n", p=P), bout).then_inc(dump_ready, 16)
            skewed(sp, NCH - 2, [(0, lambda c, u, half: load_x(c + 2, u, half + 1)),
                                 (0, lambda c, u, half: load_w(c + 2, u, half + 1))])

            sp.wait_ge(wabT_ready, 1)
            sp.dma_start(w_rows.rearrange("(n p) o -> n (p o)", p=P), wabT[:, :]).then_inc(w_stored, 16)

            def load_f(c, u, half):
                if later(c):
                    apart(sp, f_loaded[u], 16 * half)
                sp.dma_start(rf[:, bass.ds(c * FT, FT), :], xs_f[bass.ds(c, 1)].rearrange("a p k n -> (a p) k n")
                             ).then_inc(f_loaded[u], 16)

            def store_f(c, u, half):
                apart(sp, f_out, c + 1)
                if later(c):
                    apart(sp, f_stored[u], 16 * half)
                sp.dma_start(out_f[bass.ds(c, 1)].rearrange("a p k d -> (a p) k d"),
                             of[:, bass.ds(c * FT, FT), :]).then_inc(f_stored[u], 16)

            sp.wait_ge(y_added, 16 * NQ)
            skewed(sp, NF, [(0, load_f), (2, store_f)])
            for u in range(2):
                sp.wait_ge(f_stored[u], 16 * (NF // 2))

        @block.gpsimd
        def _(pool):
            made = [0]

            def fill(ins):
                made[0] += 1
                ins.then_inc(iota_made, 1)
                pool.wait_ge(iota_made, made[0])

            nc.gpsimd.memset(ones_ch, 1.0)
            nc.gpsimd.memset(eps1[:, :], EPS / XS ** 2)
            nc.gpsimd.memset(eps2[:, :], EPS * XS ** 2)
            fill(nc.gpsimd.memset(ident[:, :], 0.0))
            fill(nc.gpsimd.affine_select(out=ident[:, :], in_=ident[:, :], compare_op=ALU.not_equal, fill=1.0,
                                         base=0, pattern=[[-1, P]], channel_multiplier=1))
            nc.gpsimd.tensor_copy(ident16[:, :], ident[:, :]).then_inc(consts_made, 1)

            def residual(c, u, half):
                pool.wait_ge(x_loaded[u], 16 * (half + 1))
                if later(c):
                    pool.wait_ge(add_done, c - 1)
                nc.gpsimd.tensor_tensor(xpb[u], xin[u], bout, ALU.add).then_inc(xpb_done, 1)

            def low_part(c, u, half):
                pool.wait_ge(hi_done, c + 1)
                nc.gpsimd.tensor_tensor(xhl[u][:, :, D:2 * D], xs[u], xhl[u][:, :, 0:D], ALU.subtract
                                        ).then_inc(lo_done, 1)

            pool.wait_ge(small_loaded, 16 * 6)
            skewed(pool, NCH, [(0, residual), (3, low_part)])

            fill(nc.gpsimd.memset(ones16[:, :], 1.0))
            nc.gpsimd.affine_select(out=before16[:, :], in_=ones16[:, :], compare_op=ALU.is_gt, fill=0.0,
                                    base=0, pattern=[[1, P]], channel_multiplier=-1)
            loose = dict(allow_small_or_imprecise_dtypes=True)
            nc.gpsimd.iota(rev[:, :, :], pattern=[[0, NT], [-1, E]], base=E, channel_multiplier=0, **loose)
            nc.gpsimd.iota(tile_k[:, :, :], pattern=[[0, E], [SL, NT // 2]], base=0, channel_multiplier=0, **loose)
            nc.gpsimd.iota(iota_j[:, :, :], pattern=[[1, NJ], [0, E]], base=0, channel_multiplier=0, **loose)
            nc.gpsimd.iota(dump[:, :], pattern=[[0, NJ], [P, SUB]], base=N, channel_multiplier=1, **loose)
            nc.gpsimd.iota(code[:, 0, :], pattern=[[P, NT // 2], [0, K]], base=1, channel_multiplier=1, **loose)
            nc.gpsimd.iota(code[:, 1, :], pattern=[[-P, NT // 2], [0, K]], base=-1, channel_multiplier=-1, **loose)
            nc.gpsimd.memset(keep[:, :, 1:NT], 1.0)
            nc.gpsimd.memset(keep[:, :, 0:1], 0.0)
            nc.gpsimd.memset(one_e[:, :], 1.0).then_inc(consts_made, 1)
            pool.wait_ge(sqa_done, 1)
            nc.gpsimd.partition_all_reduce(sqa[:, :], sqm[:, :], P, bass.bass_isa.ReduceOp.max
                                           ).then_inc(sqa_done, 1)

            for u in range(2):
                pool.wait_ge(xh_stored[u], 16 * (NCH // 2))
                pool.wait_ge(xs_stored[u], 16 * (NCH // 2))
            nc.gpsimd.iota(iota_r, pattern=[[1, P], [0, NH]], base=0, channel_multiplier=0, **loose
                           ).then_inc(consts_made, 1)

            def column(idxs, kind, j, copied):
                nc.gpsimd.tensor_copy(idxs[:, :], idx[:, kind, bass.ds(j * SUB, SUB)]).then_inc(copied, 1)
                apart(pool, copied, j + 1)

            def gather(j, u, half):
                if later(j):
                    apart(pool, xg_loaded[u], 32 * half)
                column(ix[u], 0, j, ix_ready)
                if later(j):
                    apart(pool, xgT_done, j - 1)
                for q in range(SUB):
                    nc.gpsimd.indirect_dma_start(
                        out=xg[u][:, q, :], out_offset=None, in_=xh_rows,
                        in_offset=bass.IndirectOffsetOnAxis(ap=ix[u][:, q:q + 1], axis=0)
                        ).then_inc(xg_loaded[u], 16)

            def gather_w(j, u, half):
                if later(j):
                    apart(pool, wsl_loaded[u], 32 * half)
                column(iw[u], 1, j, iw_ready)
                if later(j):
                    apart(pool, ys_ready, SUB * (j - 1))
                for q in range(SUB):
                    nc.gpsimd.indirect_dma_start(
                        out=wsl[u][:, q:q + 1], out_offset=None, in_=w_rows,
                        in_offset=bass.IndirectOffsetOnAxis(ap=iw[u][:, q:q + 1], axis=0)
                        ).then_inc(wsl_loaded[u], 16)

            def scatter(j, u, half):
                if not isinstance(j, int) or j >= 1:
                    apart(pool, y_added, 32 * j)
                column(iy[u], 2, j, iy_ready)
                apart(pool, ys_ready, SUB * (j + 1))
                for q in range(SUB):
                    nc.gpsimd.indirect_dma_start(
                        out=xs_rows, out_offset=bass.IndirectOffsetOnAxis(ap=iy[u][:, q:q + 1], axis=0),
                        in_=ys[u][:, q, :], in_offset=None, compute_op=ALU.add).then_inc(y_added, 16)

            pool.wait_ge(route_ready, 1)
            pool.wait_ge(w_stored, 16)
            pool.wait_ge(dump_ready, 16)
            skewed(pool, NJ, [(0, gather), (3, scatter), (1, gather_w)])

        @block.tensor
        def _(pe):
            def transpose_x(c, u, half):
                pe.wait_ge(x_loaded[u], 16 * (half + 1))
                if later(c):
                    pe.wait_ge(bx_done, c - 1)
                for dc in range(DC):
                    for k in range(CT):
                        last = pe.transpose(bank[u][:, dc * CH + k * P:dc * CH + (k + 1) * P],
                                            xin[u][:, k, dc * P:(dc + 1) * P], ident[:, :])
                last.then_inc(xT_done, 1)

            def project(c, u, half):
                pe.wait_ge(scan_done, c + 1)
                if later(c):
                    pe.wait_ge(add_done, c - 1)
                for k in range(CT):
                    for dc in range(DC):
                        last = pe.matmul(bank[2 + u][:, k * D:(k + 1) * D], y[u][:, dc, k * P:(k + 1) * P],
                                         woT[:, dc, :], start=(dc == 0), stop=(dc == DC - 1))
                last.then_inc(proj_done, 1)

            def transpose_xs(c, u, half):
                pe.wait_ge(norm_done, c + 1)
                if later(c):
                    pe.wait_ge(xsT_done, c - 1)
                for dc in range(DC):
                    for k in range(CT):
                        last = pe.transpose(bank[4 + u][:, dc * CH + k * P:dc * CH + (k + 1) * P],
                                            xs[u][:, k, dc * P:(dc + 1) * P], ident[:, :])
                last.then_inc(t2_done, 1)

            def logits(c, u, half):
                pe.wait_ge(xsT_done, c + 1)
                for k in range(CT):
                    for dc in range(DC):
                        last = pe.matmul(bank[6][:, bass.ds((c * CT + k) * E, E)],
                                         xsT[u][:, dc * CH + k * P:dc * CH + (k + 1) * P],
                                         rwT[:, dc, :], start=(dc == 0), stop=(dc == DC - 1))
                last.then_inc(logit_done, 1)

            pe.wait_ge(consts_made, 1)
            pe.wait_ge(small_loaded, 16 * 6)
            for dc in range(DC):
                for ec in range(DC):
                    pe.transpose(bank[7][:, dc * D + ec * P:dc * D + (ec + 1) * P],
                                 wo[:, ec, dc * P:(dc + 1) * P], ident[:, :])
                last = pe.transpose(bank[6][:, dc * E:(dc + 1) * E], rw[:, dc * P:(dc + 1) * P],
                                    ident[0:E, 0:E])
            last.then_inc(param_T, 1)
            pe.wait_ge(param_ready, 1)
            skewed(pe, NCH, [(0, transpose_x), (2, project), (4, transpose_xs), (5, logits)])

            pe.wait_ge(both_ready, 1)
            pe.wait_ge(consts_made, 2)
            both_v = both[:, :, :].rearrange("p e t -> p (e t)")
            pe.matmul(bank[5][:, 0:E * NT], before16[:, :], both_v, start=True, stop=True)
            pe.matmul(bank[4][:, 0:E * NT], ones16[:, :], both_v, start=True, stop=True).then_inc(rank_done, 1)

            pe.wait_ge(wab_ready, 1)
            pe.transpose(bank[2][0:K * NT, 0:P], wab[:, :, :].rearrange("p k t -> p (k t)"), ident[:, :]
                         ).then_inc(wabT_done, 1)

            for h in range(2):
                pe.wait_ge(onehot_ready, h + 1)
                for n in range(NH):
                    last = pe.matmul(bank[n % K][:, 0:NQ], row1h[h][:, :, n], col1h[h][:, :, n],
                                     start=(h == 0 and n < K), stop=(h == 1 and n >= NH - K))
            last.then_inc(onehot_used, 1)

            def transpose_g(j, u, half):
                pe.wait_ge(xg_loaded[u], 32 * (half + 1))
                if later(j):
                    pe.wait_ge(xgT_ready, j - 1)
                t16 = bank[4 + u][:, :].bitcast(F16)
                for q in range(2 * DC):
                    for k in range(SUB):
                        last = pe.transpose(t16[:, q * SL + k * P:q * SL + (k + 1) * P],
                                            xg[u][:, k, q * P:(q + 1) * P], ident16[:, :])
                last.then_inc(xgT_done, 1)

            def up(j, u, half):
                e = pe.value_load(expert[0:1, bass.ds(j, 1)], min_val=0, max_val=E - 1)
                pe.wait_ge(w_ready, e * 2 + 2)
                if not isinstance(j, int) or j >= 1:
                    pe.wait_ge(gelu_done, 4 * j)
                pe.wait_ge(xgT_ready, j + 1)
                for hc in range(HC):
                    o = bank[hc // 2][:, (hc % 2) * SL:(hc % 2 + 1) * SL]
                    for dc in range(DC):
                        x_hi, x_lo = xgT[u][:, dc, :], xgT[u][:, DC + dc, :]
                        w_hi = w16(0, e, dc * H + hc * P, P)
                        w_lo = w16(0, e, WE + dc * H + hc * P, P)
                        pe.matmul(o, w_hi, x_hi, start=(dc == 0), stop=False)
                        pe.matmul(o, w_hi, x_lo, start=False, stop=False)
                        last = pe.matmul(o, w_lo, x_hi, start=False, stop=(dc == DC - 1))
                    if hc % 2 == 1:
                        last.then_inc(up_done, 1)

            def down(j, u, half):
                e = pe.value_load(expert[0:1, bass.ds(j, 1)], min_val=0, max_val=E - 1)
                if not isinstance(j, int) or j >= 1:
                    pe.wait_ge(ys_ready, SUB * j)
                for hc in range(HC):
                    if hc % 2 == 0:
                        pe.wait_ge(h_ready, 4 * j + hc // 2 + 1)
                    w_hi = w16(1, e, hc * D, D)
                    w_lo = w16(1, e, WE + hc * D, D)
                    for q in range(SUB):
                        c = slice(q * P, (q + 1) * P)
                        o = bank[6 + q][:, 0:D]
                        pe.matmul(o, hh[u][:, hc, c], w_hi, start=(hc == 0), stop=False)
                        pe.matmul(o, hh[u][:, hc, c], w_lo, start=False, stop=False)
                        last = pe.matmul(o, hl[u][:, hc, c], w_hi, start=False, stop=(hc == HC - 1))
                last.then_inc(down_done, 1)

            pe.wait_ge(route_ready, 1)
            skewed(pe, NJ, [(0, transpose_g), (1, up), (2, down)])

        @block.scalar
        def _(act):
            def square_w(c, u, half):
                act.wait_ge(w_loaded[u], 16 * (half + 1))
                act.wait_ge(sq_done, c)
                act.activation(junk[:, :], wbuf[u][:, bass.ds(half + 1, 1), :].rearrange("p a n -> p (a n)"),
                               ACT.Square, accum_out=sq[:, u, bass.ds(half, 1)]).then_inc(sq_done, 1)

            def scale_b(c, u, half):
                act.wait_ge(xT_done, c + 1)
                if later(c):
                    act.wait_ge(scan_done, c - 1)
                for dc in range(DC):
                    last = act.activation(bx[u][:, dc, :], bank[u][:, dc * CH:(dc + 1) * CH], ACT.Copy,
                                          scale=ab[:, 1, dc:dc + 1])
                last.then_inc(bx_done, 1)

            def deviation(c, u, half):
                act.wait_ge(mv_done, c + 1)
                if later(c):
                    act.wait_ge(rstd_done, c - 1)
                act.activation(std[u][:, :], mv[u][:, :, 1], ACT.Sqrt, bias=eps1[:, 0:1], scale=XS ** -2
                               ).then_inc(std_done, 1)

            def store_x(c, u, half):
                act.wait_ge(norm_done, c + 1)
                act.dma_start(xs_c[bass.ds(c, 1)].rearrange("a p k n -> (a p) k n"), xs[u]
                              ).then_inc(xs_stored[u], 16)
                act.wait_ge(hi_done, c + 1)
                act.wait_ge(lo_done, c + 1)
                act.dma_start(xh_c[bass.ds(c, 1)].rearrange("a p k n -> (a p) k n"), xhl[u]
                              ).then_inc(xh_stored[u], 16)

            def copy_xsT(c, u, half):
                act.wait_ge(t2_done, c + 1)
                if later(c):
                    act.wait_ge(logit_done, c - 1)
                act.activation(xsT[u], bank[4 + u][:, :], ACT.Copy).then_inc(xsT_done, 1)

            act.wait_ge(small_loaded, 16 * 6)
            act.activation(th[:, :], ab[:, 0, :], ACT.Tanh).then_inc(th_ready, 1)
            act.wait_ge(param_T, 1)
            act.activation(rwT[:, :, :].rearrange("p c e -> p (c e)"), bank[6][:, 0:DC * E], ACT.Copy)
            act.activation(woT[:, :, :].rearrange("p c e -> p (c e)"), bank[7][:, :], ACT.Copy
                           ).then_inc(param_ready, 1)
            act.wait_ge(consts_made, 1)
            skewed(act, NCH, [(0, scale_b), (3, deviation), (4, copy_xsT), (5, store_x), (2, square_w)])

            act.wait_ge(sqa_done, 2)
            act.activation(top[:, :], sqa[:, :], ACT.Sqrt).then_inc(top_done, 1)
            act.wait_ge(ex_in, 1)
            act.activation(ex[:, :, :], ex[:, :, :], ACT.Exp, scale=1.0 / XS).then_inc(ex_out, 1)

            act.wait_ge(scales_ready, 1)
            act.wait_ge(dump_ready, 16)

            def split_high(e):
                for m in range(2):
                    if e:
                        act.wait_ge(w_ready, 2 * (e - 1) + m + 1)
                    act.activation(w16(m, e, 0, WE), wbuf[m][:, e + 1, :], ACT.Copy, scale=ws[:, m:m + 1]
                                   ).then_inc(whi_done, 1)

            split_high(0)

            def gelu(j, u, half):
                for q in range(4):
                    act.wait_ge(up_done, 4 * j + q + 1)
                    if not isinstance(j, int) or j >= 1:
                        act.wait_ge(h_ready, 4 * (j - 1) + q + 1)
                    act.activation(g[:, q, :], bank[q][:, :], ACT.Gelu, scale=unz[:, 0:1]
                                   ).then_inc(gelu_done, 1)

            def copy_y(j, u, half):
                act.wait_ge(down_done, j + 1)
                act.wait_ge(wsl_loaded[u], 32 * (half + 1))
                if later(j):
                    act.wait_ge(y_added, 32 * (j - 1))
                for q in range(SUB):
                    act.activation(ys[u][:, q, :], bank[6 + q][:, 0:D], ACT.Copy, scale=wsl[u][:, q:q + 1]
                                   ).then_inc(ys_ready, 1)

            split_high(1)
            skewed(act, NJ, [(0, gelu), (None, lambda s: split_high(s + 2)), (1, copy_y)], first=E - 2)

            def f_deviation(c, u, half):
                act.wait_ge(f_mv, c + 1)
                if later(c):
                    act.wait_ge(f_rstd, c - 1)
                act.activation(fstd[u][:, :], fmv[u][:, :, 1], ACT.Sqrt, bias=eps2[:, 0:1]).then_inc(f_std, 1)

            def f_apply(c, u, half):
                apart(act, f_shift, c + 1)
                for k in range(FT):
                    last = act.activation(of[:, bass.ds(c * FT + k, 1), :].rearrange("p t d -> p (t d)"),
                                          rf[:, bass.ds(c * FT + k, 1), :].rearrange("p t d -> p (t d)"),
                                          ACT.Identity, bias=fshift[u][:, k:k + 1], scale=frstd[u][:, k:k + 1])
                last.then_inc(f_out, 1)

            skewed(act, NF, [(0, f_deviation), (1, f_apply)])

        @block.vector
        def _(dve):
            def scan(c, u, half):
                dve.wait_ge(bx_done, c + 1)
                if later(c):
                    dve.wait_ge(proj_done, c - 1)
                if u == 1:
                    dve.wait_ge(scan_done, c)
                for dc in range(DC):
                    last = dve.tensor_tensor_scan(
                        out=y[u][:, dc, :], data0=decay[:, dc, :], data1=bx[u][:, dc, :],
                        initial=0.0 if u == 0 else y[0][:, dc, CH - 1:CH], op0=ALU.mult, op1=ALU.add)
                last.then_inc(scan_done, 1)

            def add(c, u, half):
                dve.wait_ge(proj_done, c + 1)
                dve.wait_ge(xpb_done, c + 1)
                dve.tensor_tensor(res[u][:, :, :].rearrange("p k d -> p (k d)"), bank[2 + u][:, :],
                                  xpb[u][:, :, :].rearrange("p k d -> p (k d)"), ALU.add).then_inc(add_done, 1)

            def statistics(c, u, half):
                dve.wait_ge(add_done, c + 1)
                for k in range(CT):
                    last = dve.bn_stats(stats[u][:, k, :], res[u][:, k, :])
                last.then_inc(stat_done, 1)
                apart(dve, stat_done, c + 1)
                for k in range(CT):
                    last = dve.bn_aggr(mv[u][:, k, :], stats[u][:, k, :])
                last.then_inc(mv_done, 1)

            def normalise(c, u, half):
                dve.wait_ge(std_done, c + 1)
                dve.reciprocal(rstd[u][:, :], std[u][:, :]).then_inc(rstd_done, 1)
                if later(c):
                    dve.wait_ge(xs_stored[u], 16 * half)
                    dve.wait_ge(t2_done, c - 1)
                    dve.wait_ge(lo_done, c - 1)
                dve.wait_ge(rstd_done, c + 1)
                for k in range(CT):
                    last = dve.tensor_scalar(xs[u][:, k, :], res[u][:, k, :], mv[u][:, k, 0:1],
                                             rstd[u][:, k:k + 1], ALU.subtract, ALU.mult)
                last.then_inc(norm_done, 1)

            def high_part(c, u, half):
                dve.wait_ge(norm_done, c + 1)
                if later(c):
                    dve.wait_ge(xh_stored[u], 16 * half)
                dve.tensor_copy(xhl[u][:, :, 0:D], xs[u]).then_inc(hi_done, 1)

            dve.wait_ge(th_ready, 1)
            dve.wait_ge(consts_made, 1)
            for dc in range(DC):
                last = dve.tensor_scalar(decay[:, dc, :], ones_ch, th[:, dc:dc + 1], None, ALU.mult)
            last.then_inc(decay_ready, 1)
            dve.wait_ge(decay_ready, 1)
            skewed(dve, NCH, [(1, scan), (3, normalise), (2, add), (3, high_part), (2, statistics)])

            step = [0]

            def link(ins):
                step[0] += 1
                ins.then_inc(dve_step, 1)
                dve.wait_ge(dve_step, step[0])

            def over_e(v):
                return v[:, :].unsqueeze(2).to_broadcast([P, NT, E])

            def over_t(v):
                return v[:, :].unsqueeze(2).to_broadcast([P, E, NT])

            def te(v):
                return v[:, :, :].rearrange("p e t -> p t e")

            dve.wait_ge(sq_done, 2 * E)
            dve.tensor_reduce(sqm[:, :], sq[:, :, :], AX.X, ALU.max).then_inc(sqa_done, 1)

            dve.wait_ge(logit_done, NCH)
            dve.wait_ge(consts_made, 2)
            lg = bank[6][:, 0:NT * E].rearrange("p (t e) -> p t e", e=E)
            link(dve.tensor_reduce(mx[:, :], lg, AX.X, ALU.max))
            dve.tensor_tensor(ex[:, :, :], lg, over_e(mx), ALU.subtract).then_inc(ex_in, 1)

            dve.wait_ge(top_done, 1)
            link(dve.tensor_scalar(top[:, :], top[:, :], 2.0 ** -40, None, ALU.max))
            link(dve.tensor_scalar(pow2[:, :].bitcast(I32), top[:, :].bitcast(I32), 0x7F800000, None,
                                   ALU.bitwise_and))
            link(dve.reciprocal(ipow2[:, :], pow2[:, :]))
            link(dve.tensor_scalar(ws[:, :], ipow2[:, :], S_TOP, None, ALU.mult))
            dve.tensor_scalar(unz[:, :], pow2[:, 0:1], 1.0 / (S_TOP * XS), None, ALU.mult)
            link(dve.tensor_scalar(hs[:, :], ipow2[:, 0:1], S_TOP / 256, None, ALU.mult))
            dve.scalar_tensor_tensor(out=uny[:, :], in0=pow2[:, 0:1], scalar=256 * XS / S_TOP ** 2,
                                     in1=pow2[:, 1:2], op0=ALU.mult, op1=ALU.mult).then_inc(scales_ready, 1)

            dve.wait_ge(ex_out, 1)
            link(dve.tensor_reduce(sm[:, :], ex[:, :, :], AX.X, ALU.add))
            link(dve.reciprocal(rs[:, :], sm[:, :]))
            link(dve.tensor_tensor(pr[:, :, :], ex[:, :, :], over_e(rs), ALU.mult))
            link(dve.tensor_reduce(p1[:, :], pr[:, :, :], AX.X, ALU.max))
            link(dve.tensor_tensor(eq[:, :, :], pr[:, :, :], over_e(p1), ALU.is_equal))
            link(dve.tensor_tensor(eq[:, :, :], eq[:, :, :], rev[:, :, :], ALU.mult))
            link(dve.tensor_reduce(k1[:, :], eq[:, :, :], AX.X, ALU.max))
            link(dve.tensor_tensor(oh1[:, :, :], rev[:, :, :], over_e(k1), ALU.is_equal))
            link(dve.scalar_tensor_tensor(out=pr[:, :, :], in0=oh1[:, :, :], scalar=-4.0, in1=pr[:, :, :],
                                          op0=ALU.mult, op1=ALU.add))
            link(dve.tensor_reduce(p2[:, :], pr[:, :, :], AX.X, ALU.max))
            link(dve.tensor_tensor(eq[:, :, :], pr[:, :, :], over_e(p2), ALU.is_equal))
            link(dve.tensor_tensor(eq[:, :, :], eq[:, :, :], rev[:, :, :], ALU.mult))
            link(dve.tensor_reduce(k1[:, :], eq[:, :, :], AX.X, ALU.max))
            link(dve.tensor_tensor(oh2[:, :, :], rev[:, :, :], over_e(k1), ALU.is_equal))
            dve.tensor_tensor(te(both), oh1[:, :, :], oh2[:, :, :], ALU.add).then_inc(both_ready, 1)
            link(dve.tensor_tensor(sm[:, :], p1[:, :], p2[:, :], ALU.add))
            link(dve.reciprocal(rs[:, :], sm[:, :]))
            link(dve.tensor_scalar(rs[:, :], rs[:, :], uny[:, 0:1], None, ALU.mult))
            dve.tensor_tensor(wab[:, 0, :], p1[:, :], rs[:, :], ALU.mult)
            dve.tensor_tensor(wab[:, 1, :], p2[:, :], rs[:, :], ALU.mult).then_inc(wab_ready, 1)

            dve.wait_ge(rank_done, 1)
            link(dve.tensor_copy(ptot[:, :, :].rearrange("p e t -> p (e t)"), bank[4][:, 0:E * NT]))
            link(dve.tensor_tensor_scan(out=incl[:, :, :].rearrange("p e t -> p (e t)"),
                                        data0=keep[:, :, :].rearrange("p e t -> p (e t)"),
                                        data1=ptot[:, :, :].rearrange("p e t -> p (e t)"),
                                        initial=0.0, op0=ALU.mult, op1=ALU.add))
            link(dve.tensor_copy(cnt[:, :], incl[:, :, NT - 1]))
            few = slot[:, :, 0:NT // 2]
            link(dve.tensor_tensor(few, tile_k[:, :, :], cnt[:, :].unsqueeze(2).to_broadcast([P, E, NT // 2]),
                                   ALU.is_lt))
            link(dve.tensor_reduce(nt[:, :], few, AX.X, ALU.add))
            link(dve.tensor_scalar(nt[:, :], nt[:, :], 1.0, None, ALU.max))
            link(dve.tensor_tensor_scan(out=endt[:, :], data0=one_e[:, :], data1=nt[:, :], initial=0.0,
                                        op0=ALU.mult, op1=ALU.add))
            link(dve.tensor_tensor(base[:, :], endt[:, :], nt[:, :], ALU.subtract))
            link(dve.tensor_scalar(base[:, :], base[:, :], float(SL), None, ALU.mult))
            link(dve.tensor_tensor(incl[:, :, :], incl[:, :, :], ptot[:, :, :], ALU.subtract))
            link(dve.tensor_tensor(incl[:, :, :], incl[:, :, :], over_t(base), ALU.add))
            link(dve.tensor_tensor(slot[:, :, :].rearrange("p e t -> p (e t)"), bank[5][:, 0:E * NT],
                                   incl[:, :, :].rearrange("p e t -> p (e t)"), ALU.add))
            dve.tensor_tensor(eq[:, :, :], oh1[:, :, :], te(slot), ALU.mult)
            link(dve.tensor_tensor(ex[:, :, :], oh2[:, :, :], te(slot), ALU.mult))
            dve.tensor_reduce(sl[:, 0, :], eq[:, :, :], AX.X, ALU.add)
            link(dve.tensor_reduce(sl[:, 1, :], ex[:, :, :], AX.X, ALU.add))
            link(dve.tensor_copy(sli[:, :, :], sl[:, :, :]))
            dve.tensor_scalar(slr_i[:, :, :], sli[:, :, :], P - 1, None, ALU.bitwise_and)
            link(dve.tensor_scalar(slj_i[:, :, :], sli[:, :, :], 7, None, ALU.logical_shift_right))
            tk = "p (t k) -> p k t"
            dve.tensor_copy(slr[:, :].rearrange(tk, k=K), slr_i[:, :, :])
            link(dve.tensor_copy(slj[:, :].rearrange(tk, k=K), slj_i[:, :, :]))

            dve.wait_ge(consts_made, 3)
            for h in range(2):
                def over(v, n):
                    return v.unsqueeze(1).to_broadcast([P, n, NH])

                link(dve.tensor_tensor(col1h[h], iota_r[:, 0:NQ, :], over(slj[:, h * NH:(h + 1) * NH], NQ),
                                       ALU.is_equal))
                dve.tensor_tensor(col1h[h], col1h[h], over(code[:, h, :], NQ), ALU.mult)
                dve.tensor_tensor(row1h[h], iota_r, over(slr[:, h * NH:(h + 1) * NH], P), ALU.is_equal
                                  ).then_inc(onehot_ready, 1)

            link(dve.tensor_tensor(past[:, :, :], iota_j[0:1, :, :],
                                   endt[0:1, :].unsqueeze(1).to_broadcast([1, NJ, E]), ALU.is_ge))
            link(dve.tensor_reduce(expf[:, :], past[:, :, :], AX.X, ALU.add))
            dve.tensor_scalar(expert[:, 0:NJ], expf[:, :], float(E - 1), None, ALU.min)

            dve.wait_ge(wabT_done, 1)
            dve.tensor_copy(wabT[:, :], bank[2][0:K * NT, 0:P]).then_inc(wabT_ready, 1)

            def split_low(e):
                for m in range(2):
                    dve.wait_ge(whi_done, 2 * e + m + 1)
                    dve.scalar_tensor_tensor(out=w16(m, e, WE, WE), in0=wbuf[m][:, e + 1, :],
                                             scalar=ws[:, m:m + 1], in1=w16(m, e, 0, WE),
                                             op0=ALU.mult, op1=ALU.subtract).then_inc(w_ready, 1)

            dve.wait_ge(onehot_used, 1)
            link(dve.tensor_copy(v0[:, :], bank[0][:, 0:NQ]))
            dve.tensor_scalar(vk[:, :], bank[1][:, 0:NQ], 0.0, float(N), ALU.not_equal, ALU.mult)
            link(dve.tensor_tensor(vs[:, :], bank[1][:, 0:NQ], v0[:, :], ALU.add))
            dve.tensor_scalar(vneg[:, :], vs[:, :], 0.0, float(N // 2), ALU.is_lt, ALU.mult)
            dve.scalar_tensor_tensor(out=v0[:, :], in0=vs[:, :], scalar=0.0, in1=dump[:, :],
                                     op0=ALU.is_equal, op1=ALU.mult)
            link(dve.scalar_tensor_tensor(out=va[:, :], in0=vs[:, :], scalar=-1.0, in1=vs[:, :],
                                          op0=ALU.mult, op1=ALU.max))
            link(dve.tensor_tensor(va[:, :], va[:, :], vneg[:, :], ALU.add))
            link(dve.tensor_scalar(tok[:, :], va[:, :], -1.0, 0.0, ALU.add, ALU.max))
            dve.tensor_copy(idx[:, 0, :], tok[:, :])
            dve.tensor_tensor(idx[:, 1, :], tok[:, :], vk[:, :], ALU.add)
            dve.tensor_tensor(idx[:, 2, :], tok[:, :], v0[:, :], ALU.add).then_inc(route_ready, 1)

            split_low(0)

            def columns(j, u, half):
                dve.wait_ge(xgT_done, j + 1)
                if later(j):
                    dve.wait_ge(up_done, 4 * (j - 1))
                dve.tensor_copy(xgT[u].rearrange("p q s -> p (q s)"), bank[4 + u][:, :].bitcast(F16)
                                ).then_inc(xgT_ready, 1)

            def split(j, u, half):
                if later(j):
                    dve.wait_ge(down_done, j - 1)
                for q in range(4):
                    hi = hh[u][:, 2 * q:2 * q + 2, :].rearrange("p c s -> p (c s)")
                    lo = hl[u][:, 2 * q:2 * q + 2, :].rearrange("p c s -> p (c s)")
                    dve.wait_ge(gelu_done, 4 * j + q + 1)
                    dve.tensor_scalar(hi, g[:, q, :], hs[:, 0:1], None, ALU.mult).then_inc(hh_done, 1)
                    dve.wait_ge(hh_done, 4 * j + q + 1)
                    dve.scalar_tensor_tensor(out=lo, in0=g[:, q, :], scalar=hs[:, 0:1], in1=hi,
                                             op0=ALU.mult, op1=ALU.subtract).then_inc(h_ready, 1)

            skewed(dve, NJ, [(0, columns), (1, split), (None, lambda s: split_low(s + 1))], first=E - 1)

            def f_statistics(c, u, half):
                apart(dve, f_loaded[u], 16 * (half + 1))
                if later(c):
                    apart(dve, f_std, c - 1)
                for k in range(FT):
                    last = dve.bn_stats(fstats[u][:, k, :],
                                        rf[:, bass.ds(c * FT + k, 1), :].rearrange("p t d -> p (t d)"))
                last.then_inc(f_stat, 1)
                apart(dve, f_stat, c + 1)
                for k in range(FT):
                    last = dve.bn_aggr(fmv[u][:, k, :], fstats[u][:, k, :])
                last.then_inc(f_mv, 1)

            def f_scale(c, u, half):
                dve.wait_ge(f_std, c + 1)
                if later(c):
                    dve.wait_ge(f_out, c - 1)
                dve.reciprocal(frstd[u][:, :], fstd[u][:, :]).then_inc(f_rstd, 1)
                dve.wait_ge(f_rstd, c + 1)
                dve.scalar_tensor_tensor(out=fshift[u][:, :], in0=fmv[u][:, :, 0], scalar=-1.0,
                                         in1=frstd[u][:, :], op0=ALU.mult, op1=ALU.mult).then_inc(f_shift, 1)

            skewed(dve, NF, [(0, f_statistics), (1, f_scale)])


_INS = ["L0_attn_x", "L0_attn_a", "L0_attn_b", "L0_attn_w_out", "L0_attn_b_out", "L0_ffn_router_w", "L0_ffn_w1",
        "L0_ffn_w2"]


def kernel(**inputs):
    import numpy as np
    import concourse.bacc as bacc
    from concourse.bass_utils import run_bass_kernel_spmd

    nc = bacc.Bacc("TRN2", target_bir_lowering=False, num_devices=1)
    arrays, args = {}, []
    for name in _INS:
        v = np.ascontiguousarray(inputs[name])
        arrays[name] = v
        args.append(nc.dram_tensor(name, v.shape, mybir.dt.from_np(v.dtype), kind="ExternalInput").ap())
    B, S, D = inputs["L0_attn_x"].shape
    args.append(nc.dram_tensor("out", (B, S, D), F32, kind="ExternalOutput").ap())
    args.append(nc.dram_tensor("xh_rows", (B * S, 2 * D), F16, kind="Internal").ap())
    args.append(nc.dram_tensor("xs_rows", (B * S + 256, D), F32, kind="Internal").ap())
    args.append(nc.dram_tensor("w_rows", (2 * B * S, 1), F32, kind="Internal").ap())
    build(nc, *args)
    r = run_bass_kernel_spmd(nc, [arrays], core_ids=[0])
    return r.results[0]["out"]
```

```python
from contextlib import ExitStack

import concourse.bass as bass
from concourse import mybir

F32 = mybir.dt.float32
F16 = mybir.dt.float16
BF16 = mybir.dt.bfloat16
I32 = mybir.dt.int32
U32 = mybir.dt.uint32
ALU = mybir.AluOpType
ACT = mybir.ActivationFunctionType
AX = mybir.AxisListType

P = 128
EPS = 1e-5
XS = 2048.0
S_TOP = 16384.0


def later(c, ring=2):
    return not isinstance(c, int) or c >= ring


def skewed(eng, n, stages, first=0, last=0, there=None, unroll=2):
    looped = [s for s in stages if s[0] is not None]
    deepest = max(lag for lag, _ in looped)
    lo = max(deepest + 2, first)
    lo += -lo % unroll
    hi = n - last
    hi -= (hi - lo) % unroll

    def straight(steps):
        for s in steps:
            for lag, stage in stages:
                if lag is None:
                    if s < first:
                        stage(s)
                elif n - last <= s - lag < n:
                    with eng.If(there > s - lag):
                        stage(s - lag, (s - lag) % unroll, (s - lag) // unroll)
                elif 0 <= s - lag < n - last:
                    stage(s - lag, (s - lag) % unroll, (s - lag) // unroll)

    straight(range(lo))
    if hi > lo:
        with eng.Fori(lo // unroll, hi // unroll) as i:
            for v in range(unroll):
                for lag, stage in looped:
                    stage(i * unroll + (v - lag), (v - lag) % unroll, i + (v - lag) // unroll)
    straight(range(hi, n + deepest))


def build(nc, x, a, b, w_out, b_out, router_w, w1, w2, out, xh_rows, xs_rows, w_rows):
    B, S, D = x.shape
    E, _, H = w1.shape
    N = B * S
    NT = N // P
    DC = D // P
    HC = H // P
    K = 2
    CT = 2
    CH = CT * P
    NCH = N // CH
    RING = 4
    SUB = 2
    SL = SUB * P
    NJ = (K * N - E) // SL + E
    NQ = NJ * SUB
    LAST = 5
    FT = 4
    NF = NT // FT
    NH = NT // 2 * K
    WE = DC * H
    assert S == 2 * CH == FT * P and WE == HC * D == RING * CT * D and DC == 2 and NT * E <= 512

    x_c = x.rearrange("b (h k p) d -> (b h) p k d", h=2, p=P)
    out_f = out.rearrange("b (k p) d -> b p k d", p=P)
    xh_c = xh_rows.rearrange("(c k p) n -> c p k n", k=CT, p=P)
    xs_c = xs_rows[0:N, :].rearrange("(c k p) n -> c p k n", k=CT, p=P)
    xs_f = xs_rows[0:N, :].rearrange("(c k p) n -> c p k n", k=FT, p=P)
    w_c = [w1.rearrange("e (c p) h -> e p c h", p=P), w2.rearrange("e (c p) n -> e p c n", p=P)]

    with ExitStack() as ctx:
        def sb(name, shape, dt):
            return ctx.enter_context(nc.sbuf_tensor(name, shape, dt))

        def sem(name):
            return ctx.enter_context(nc.semaphore(name))

        def pair(name, n=2):
            return [sem(f"{name}{u}") for u in range(n)]

        bank = [ctx.enter_context(nc.psum_tensor(f"bank{i}", [P, 512], F32)) for i in range(8)]

        wbuf = [sb(f"wbuf{m}", [P, E + 1, WE], F32) for m in range(2)]
        spare = [w[:, 0, :] for w in wbuf]
        rows = [wbuf[1][:, E // 2 + 1 + i, :].rearrange("p (r k d) -> p r k d", r=RING, k=CT) for i in range(4)]
        wpart = [w[:, :, :].rearrange("p e n -> p (e n)").bitcast(F16) for w in wbuf]

        def w16(m, e, off, n):
            return wpart[m][:, bass.ds(e * (2 * WE) + off, n)]

        ident = sb("ident", [P, P], F32)
        minus16 = sb("minus16", [P, P], F16)
        from16 = sb("from16", [P, P], F16)
        ones16 = sb("ones16", [P, P], F16)
        rev = sb("rev", [P, NT, E], F32)
        keep = sb("keep", [P, E, NT], F32)
        tile_k = sb("tile_k", [P, E, NT // 2], F32)
        code = sb("code", [P, 2, NH], F16)
        iota_j = sb("iota_j", [P, NJ, E], F32)
        dump = sb("dump", [P, NQ], F32)
        one_e = sb("one_e", [P, E], F32)

        ab = sb("ab", [P, 2, DC], F32)
        th = sb("th", [P, DC], F32)
        decay = spare[1][:, 0:512].rearrange("p (c n) -> p c n", c=DC)
        bout = spare[1][:, 512:1024].rearrange("p (c n) -> p c n", c=CT)
        woT = spare[1][:, 1024:1536].rearrange("p (c n) -> p c n", c=DC)
        wo = spare[0][:, 0:512].rearrange("p (c n) -> p c n", c=DC)
        rw = spare[0][0:E, 512:512 + D]
        ones_ch = spare[0][:, 768:768 + CH]
        rwT = sb("rwT", [P, DC, E], F32)

        arena = sb("arena", [P, 9216], F32)
        taken = [0]

        def part(shape, dt=F32):
            words = 1
            for d in shape:
                words *= d
            words = words * (1 if dt == F32 else 0.5)
            v = arena[:, int(taken[0]):int(taken[0] + words)]
            taken[0] += words
            assert taken[0] <= 9216
            v = v if dt == F32 else v.bitcast(dt)
            names = "abcd"[:len(shape)]
            return v.rearrange(f"p ({' '.join(names)}) -> p {' '.join(names)}", **dict(zip(names, shape)))

        def parts(shape, dt=F32):
            return [part(shape, dt) for _ in range(2)]

        def ring(name, shape, dt):
            return [sb(f"{name}{u}", shape, dt) for u in range(2)]

        xin, xpb, xs = ([v[:, r] for r in range(RING)] for v in rows[:3])
        xhl = [rows[3][:, r].rearrange("p k d -> p (k d)").bitcast(F16).rearrange("p (k d) -> p k d", k=CT)
               for r in range(RING)]
        bx, y, res, xsT = parts([DC, CH]), parts([DC, CH]), parts([CT, D]), parts([DC * CH])
        stats = ring("stats", [P, CT, 6], F32)
        mv = ring("mv", [P, CT, 2], F32)
        std = ring("std", [P, CT], F32)
        rstd = ring("rstd", [P, CT], F32)
        eps1 = sb("eps1", [P, 1], F32)
        eps2 = sb("eps2", [P, 1], F32)

        junk = spare[0][:, 1024:2048].bitcast(BF16)
        sq = sb("sq", [P, 2, E], F32)
        sqm = sb("sqm", [P, 2], F32)
        sqa = sb("sqa", [P, 2], F32)
        top = sb("top", [P, 2], F32)
        pow2 = sb("pow2", [P, 2], F32)
        ipow2 = sb("ipow2", [P, 2], F32)
        ws = sb("ws", [P, 2], F32)
        hs = sb("hs", [P, 1], F32)
        unz = sb("unz", [P, 1], F32)
        uny = sb("uny", [P, 1], F32)

        def rt(name, shape=(P, NT, E), dt=F32):
            return sb(name, list(shape), dt)

        ex, pr = rt("ex"), rt("pr")
        eq, oh1, oh2 = rt("eq"), rt("oh1"), rt("oh2")
        mx, sm, rs = rt("mx", (P, NT)), rt("sm", (P, NT)), rt("rs", (P, NT))
        p1, p2, k1 = rt("p1", (P, NT)), rt("p2", (P, NT)), rt("k1", (P, NT))
        wab = rt("wab", (P, K, NT))
        both = rt("both", (P, E, NT), F16)
        incl, slot = rt("incl", (P, E, NT)), rt("slot", (P, E, NT))
        cnt, nt, endt, base = rt("cnt", (P, E)), rt("nt", (P, E)), rt("endt", (P, E)), rt("base", (P, E))
        sl = rt("sl", (P, K, NT))
        sli, slr_i, slj_i = (rt(n, (P, K, NT), I32) for n in ("sli", "slr_i", "slj_i"))
        slr, slj = rt("slr", (P, NT * K), F16), rt("slj", (P, NT * K), F16)
        past = rt("past", (1, NJ, E))
        expf = rt("expf", (1, NJ))
        expert = rt("expert", (1, NJ + 1), I32)
        v0, vs, va, vneg, vk = (rt(n, (P, NQ)) for n in ("v0", "vs", "va", "vneg", "vk"))
        used = rt("used", (1, 1), I32)
        tok = rt("tok", (P, NQ))
        idx = rt("idx", (P, 3, NQ), U32)
        wabT = rt("wabT", (K * NT, P))
        taken[0] = 0
        row1h = parts([P, NH], F16)
        iota_r = part([P, NH], F16)
        col1h = parts([NQ, NH], F16)

        taken[0] = 0
        xg = parts([SUB, 2 * D], F16)
        xgT = parts([2 * DC, SL], F16)
        g = part([4, 512])
        hh = parts([HC, SL], F16)
        hl = parts([HC, SL], F16)
        ys = parts([SUB, D])
        ix = ring("ix", [P, SUB], U32)
        iw = ring("iw", [P, SUB], U32)
        iy = ring("iy", [P, SUB], U32)
        wsl = ring("wsl", [P, SUB], F32)

        rf = wbuf[0][:, :, :].rearrange("p e n -> p (e n)")[:, 0:NT * D].rearrange("p (t d) -> p t d", d=D)
        of = wbuf[1][:, :, :].rearrange("p e n -> p (e n)")[:, 0:NT * D].rearrange("p (t d) -> p t d", d=D)
        fstats = ring("fstats", [P, FT, 6], F32)
        fmv = ring("fmv", [P, FT, 2], F32)
        fstd = ring("fstd", [P, FT], F32)
        frstd = ring("frstd", [P, FT], F32)
        fshift = ring("fshift", [P, FT], F32)

        small_loaded = sem("small_loaded")
        consts_made = sem("consts_made")
        iota_made = sem("iota_made")
        th_ready = sem("th_ready")
        decay_ready = sem("decay_ready")
        param_T = sem("param_T")
        param_ready = sem("param_ready")
        x_loaded = pair("x_loaded", RING)
        xT_done = sem("xT_done")
        bx_done = sem("bx_done")
        scan_done = sem("scan_done")
        proj_done = sem("proj_done")
        xpb_done = sem("xpb_done")
        add_done = sem("add_done")
        stat_done = sem("stat_done")
        mv_done = sem("mv_done")
        std_done = sem("std_done")
        rstd_done = sem("rstd_done")
        norm_done = sem("norm_done")
        hi_done = sem("hi_done")
        lo_done = sem("lo_done")
        xh_stored = pair("xh_stored", RING)
        xs_stored = pair("xs_stored", RING)
        t2_done = sem("t2_done")
        xsT_done = sem("xsT_done")
        logit_done = sem("logit_done")
        w1_loaded = sem("w1_loaded")
        w2_loaded = pair("w2_loaded")
        sq_done = sem("sq_done")
        sqa_done = sem("sqa_done")
        top_done = sem("top_done")
        scales_ready = sem("scales_ready")
        whi_done = sem("whi_done")
        w_ready = sem("w_ready")
        dve_step = sem("dve_step")
        ex_in = sem("ex_in")
        ex_out = sem("ex_out")
        both_ready = sem("both_ready")
        rank_done = sem("rank_done")
        onehot_ready = sem("onehot_ready")
        onehot_used = sem("onehot_used")
        place_done = sem("place_done")
        route_ready = sem("route_ready")
        tables_ready = sem("tables_ready")
        ix_ready = sem("ix_ready")
        iw_ready = sem("iw_ready")
        iy_ready = sem("iy_ready")
        wsl_loaded = pair("wsl_loaded")
        wabT_done = sem("wabT_done")
        wab_ready = sem("wab_ready")
        wabT_ready = sem("wabT_ready")
        w_stored = sem("w_stored")
        dump_ready = sem("dump_ready")
        xg_loaded = pair("xg_loaded")
        xgT_ready = pair("xgT_ready")
        up_done = sem("up_done")
        gelu_done = sem("gelu_done")
        hh_done = sem("hh_done")
        h_ready = sem("h_ready")
        down_done = sem("down_done")
        ys_ready = sem("ys_ready")
        y_added = sem("y_added")
        all_added = sem("all_added")
        f_loaded = pair("f_loaded")
        f_stat = sem("f_stat")
        f_mv = sem("f_mv")
        f_std = sem("f_std")
        f_rstd = sem("f_rstd")
        f_shift = sem("f_shift")
        f_out = pair("f_out")
        f_stored = pair("f_stored")

        def apart(eng, semaphore, value):
            eng.wait_ge(semaphore, value)
            eng.sem_inc(passed, 1)

        def tiles_used(eng):
            return eng.value_load(used[0:1, 0:1], min_val=1, max_val=NJ)

        passed = sem("passed")
        block = ctx.enter_context(nc.Block())

        @block.sync
        def _(sp):
            def load_x(c, u, quarter):
                if later(c, RING):
                    sp.wait_ge(xT_done, c - 3)
                    apart(sp, xpb_done, c - 3)
                sp.dma_start(xin[u], x_c[bass.ds(c, 1)].rearrange("a p k d -> (a p) k d")
                             ).then_inc(x_loaded[u], 16)

            def load_matrix(m, e, loaded):
                place = wbuf[m][:, bass.ds(e + 1, 1), :].rearrange("p a (c n) -> p (a c) n", c=w_c[m].shape[2])
                sp.dma_start(place, w_c[m][bass.ds(e, 1)].rearrange("a p c n -> (a p) c n")
                             ).then_inc(loaded, 16)

            def load_w1(c, u, quarter):
                if u % 2 == 0:
                    e = quarter * 2 + u // 2
                    if later(e, 1):
                        apart(sp, w1_loaded, 16 * e)
                    load_matrix(0, e, w1_loaded)

            def load_w2(e):
                if e >= 2:
                    sp.wait_ge(w2_loaded[e % 2], 16 * (e // 2))
                load_matrix(1, e, w2_loaded[e % 2])

            skewed(sp, NCH, [(0, load_x), (4, load_w1)], unroll=RING)
            sp.wait_ge(norm_done, NCH - RING)
            for e in range(E // 2):
                load_w2(e)

            sp.wait_ge(xT_done, NCH)
            sp.wait_ge(xpb_done, NCH)
            load_w2(4)
            sp.wait_ge(add_done, NCH)
            load_w2(5)
            sp.wait_ge(t2_done, NCH)
            sp.wait_ge(lo_done, NCH)
            for r in range(RING):
                sp.wait_ge(xs_stored[r], 16 * (NCH // RING))
            load_w2(6)
            for r in range(RING):
                sp.wait_ge(xh_stored[r], 16 * (NCH // RING))
            load_w2(7)

            sp.wait_ge(wabT_ready, 1)
            sp.dma_start(w_rows.rearrange("(n p) o -> n (p o)", p=P), wabT[:, :]).then_inc(w_stored, 16)

            def transpose_g(j, u, half):
                apart(sp, xg_loaded[u], 32 * (half + 1))
                if later(j):
                    apart(sp, up_done, 4 * (j - 1))
                for q in range(SUB):
                    sp.dma_start_transpose(xgT[u][:, :, q * P:(q + 1) * P], xg[u][:, q, :]
                                           ).then_inc(xgT_ready[u], 16)

            sp.wait_ge(route_ready, 1)
            skewed(sp, NJ, [(0, transpose_g)], last=LAST, there=tiles_used(sp))
            def load_f(c, u, half):
                if later(c):
                    sp.wait_ge(f_loaded[u], 16 * half)
                sp.dma_start(rf[:, bass.ds(c * FT, FT), :], xs_f[bass.ds(c, 1)].rearrange("a p k n -> (a p) k n")
                             ).then_inc(f_loaded[u], 16)

            def store_f(c, u, half):
                for by in f_out:
                    sp.wait_ge(by, c + 1)
                if later(c):
                    sp.wait_ge(f_stored[u], 16 * half)
                sp.dma_start(out_f[bass.ds(c, 1)].rearrange("a p k d -> (a p) k d"),
                             of[:, bass.ds(c * FT, FT), :]).then_inc(f_stored[u], 16)

            sp.wait_ge(all_added, 1)
            skewed(sp, NF, [(0, load_f)], first=NF)
            skewed(sp, NF, [(0, store_f)], first=NF)
            for u in range(2):
                sp.wait_ge(f_stored[u], 16 * (NF // 2))

        @block.gpsimd
        def _(pool):
            made = [0]

            def fill(ins):
                made[0] += 1
                ins.then_inc(iota_made, 1)
                pool.wait_ge(iota_made, made[0])

            nc.gpsimd.memset(ones_ch, 1.0)
            nc.gpsimd.memset(eps1[:, :], EPS / XS ** 2)
            nc.gpsimd.memset(eps2[:, :], EPS * XS ** 2)
            fill(nc.gpsimd.memset(ident[:, :], 0.0))
            nc.gpsimd.affine_select(out=ident[:, :], in_=ident[:, :], compare_op=ALU.not_equal, fill=1.0,
                                    base=0, pattern=[[-1, P]], channel_multiplier=1).then_inc(consts_made, 1)

            nc.gpsimd.memset(ones16[:, :], 1.0)
            fill(nc.gpsimd.memset(minus16[:, :], -1.0))
            nc.gpsimd.affine_select(out=from16[:, :], in_=minus16[:, :], compare_op=ALU.is_ge, fill=0.0,
                                    base=0, pattern=[[-1, P]], channel_multiplier=1)
            loose = dict(allow_small_or_imprecise_dtypes=True)
            nc.gpsimd.iota(rev[:, :, :], pattern=[[0, NT], [-1, E]], base=E, channel_multiplier=0, **loose)
            nc.gpsimd.iota(tile_k[:, :, :], pattern=[[0, E], [SL, NT // 2]], base=0, channel_multiplier=0, **loose)
            nc.gpsimd.iota(iota_j[:, :, :], pattern=[[1, NJ], [0, E]], base=0, channel_multiplier=0, **loose)
            nc.gpsimd.iota(dump[:, :], pattern=[[0, NJ], [P, SUB]], base=N, channel_multiplier=1, **loose)
            nc.gpsimd.iota(code[:, 0, :], pattern=[[P, NT // 2], [0, K]], base=1, channel_multiplier=1, **loose)
            nc.gpsimd.iota(code[:, 1, :], pattern=[[-P, NT // 2], [0, K]], base=-1, channel_multiplier=-1, **loose)
            nc.gpsimd.memset(keep[:, :, 1:NT], 1.0)
            nc.gpsimd.memset(keep[:, :, 0:1], 0.0)
            nc.gpsimd.memset(one_e[:, :], 1.0).then_inc(consts_made, 1)

            def residual(c, u, quarter):
                pool.wait_ge(x_loaded[u], 16 * (quarter + 1))
                if later(c, RING):
                    pool.wait_ge(add_done, c - 3)
                nc.gpsimd.tensor_tensor(xpb[u], xin[u], bout, ALU.add).then_inc(xpb_done, 1)

            def low_part(c, u, quarter):
                pool.wait_ge(hi_done, c + 1)
                nc.gpsimd.tensor_tensor(xhl[u][:, :, D:2 * D], xs[u], xhl[u][:, :, 0:D], ALU.subtract
                                        ).then_inc(lo_done, 1)

            pool.wait_ge(small_loaded, 16 * 6)
            skewed(pool, NCH, [(0, residual), (4, low_part)], unroll=RING)

            nc.gpsimd.iota(iota_r, pattern=[[1, P], [0, NH]], base=0, channel_multiplier=0, **loose
                           ).then_inc(consts_made, 1)

            pool.wait_ge(sqa_done, 1)
            nc.gpsimd.partition_all_reduce(sqa[:, :], sqm[:, :], P, bass.bass_isa.ReduceOp.max
                                           ).then_inc(sqa_done, 1)

            def column(idxs, kind, j, copied):
                nc.gpsimd.tensor_copy(idxs[:, :], idx[:, kind, bass.ds(j * SUB, SUB)]).then_inc(copied, 1)
                apart(pool, copied, j + 1)

            def gather(j, u, half):
                if later(j):
                    apart(pool, xg_loaded[u], 32 * half)
                column(ix[u], 0, j, ix_ready)
                if later(j):
                    apart(pool, xgT_ready[u], 32 * half)
                for q in range(SUB):
                    nc.gpsimd.indirect_dma_start(
                        out=xg[u][:, q, :], out_offset=None, in_=xh_rows,
                        in_offset=bass.IndirectOffsetOnAxis(ap=ix[u][:, q:q + 1], axis=0)
                        ).then_inc(xg_loaded[u], 16)

            def gather_w(j, u, half):
                if isinstance(j, int) and j == 0:
                    pool.wait_ge(w_stored, 16)
                if later(j):
                    apart(pool, wsl_loaded[u], 32 * half)
                column(iw[u], 1, j, iw_ready)
                if later(j):
                    apart(pool, ys_ready, SUB * (j - 1))
                for q in range(SUB):
                    nc.gpsimd.indirect_dma_start(
                        out=wsl[u][:, q:q + 1], out_offset=None, in_=w_rows,
                        in_offset=bass.IndirectOffsetOnAxis(ap=iw[u][:, q:q + 1], axis=0)
                        ).then_inc(wsl_loaded[u], 16)

            def scatter(j, u, half):
                if not isinstance(j, int) or j >= 1:
                    apart(pool, y_added, 32 * j)
                column(iy[u], 2, j, iy_ready)
                apart(pool, ys_ready, SUB * (j + 1))
                for q in range(SUB):
                    nc.gpsimd.indirect_dma_start(
                        out=xs_rows, out_offset=bass.IndirectOffsetOnAxis(ap=iy[u][:, q:q + 1], axis=0),
                        in_=ys[u][:, q, :], in_offset=None, compute_op=ALU.add).then_inc(y_added, 16)

            for r in range(RING):
                pool.wait_ge(xh_stored[r], 16 * (NCH // RING))
                pool.wait_ge(xs_stored[r], 16 * (NCH // RING))
            pool.wait_ge(route_ready, 1)
            pool.wait_ge(dump_ready, 16)
            tiles = tiles_used(pool)
            skewed(pool, NJ, [(0, gather), (3, scatter), (1, gather_w)], last=LAST, there=tiles)
            pool.wait_ge(y_added, tiles * 32)
            pool.sem_inc(all_added, 1)

            def f_apply_last(c, u, half):
                pool.wait_ge(f_loaded[u], 16 * (half + 1))
                pool.wait_ge(f_rstd, c + 1)
                nc.gpsimd.tensor_scalar(of[:, c * FT + FT - 1, :], rf[:, c * FT + FT - 1, :],
                                        fmv[u][:, FT - 1, 0:1], frstd[u][:, FT - 1:FT], ALU.subtract, ALU.mult
                                        ).then_inc(f_out[1], 1)

            skewed(pool, NF, [(0, f_apply_last)], first=NF)

        @block.tensor
        def _(pe):
            def transpose_x(c, u, quarter):
                pe.wait_ge(x_loaded[u], 16 * (quarter + 1))
                if later(c):
                    pe.wait_ge(bx_done, c - 1)
                for dc in range(DC):
                    for k in range(CT):
                        last = pe.transpose(bank[u % 2][:, dc * CH + k * P:dc * CH + (k + 1) * P],
                                            xin[u][:, k, dc * P:(dc + 1) * P], ident[:, :])
                last.then_inc(xT_done, 1)

            def project(c, r, quarter):
                u = r % 2
                pe.wait_ge(scan_done, c + 1)
                if later(c):
                    pe.wait_ge(add_done, c - 1)
                for k in range(CT):
                    for dc in range(DC):
                        last = pe.matmul(bank[2 + u][:, k * D:(k + 1) * D], y[u][:, dc, k * P:(k + 1) * P],
                                         woT[:, dc, :], start=(dc == 0), stop=(dc == DC - 1))
                last.then_inc(proj_done, 1)

            def transpose_xs(c, u, quarter):
                pe.wait_ge(norm_done, c + 1)
                if later(c):
                    pe.wait_ge(xsT_done, c - 1)
                for dc in range(DC):
                    for k in range(CT):
                        last = pe.transpose(bank[4 + u % 2][:, dc * CH + k * P:dc * CH + (k + 1) * P],
                                            xs[u][:, k, dc * P:(dc + 1) * P], ident[:, :])
                last.then_inc(t2_done, 1)

            def logits(c, r, quarter):
                u = r % 2
                pe.wait_ge(xsT_done, c + 1)
                for k in range(CT):
                    for dc in range(DC):
                        last = pe.matmul(bank[6][:, bass.ds((c * CT + k) * E, E)],
                                         xsT[u][:, dc * CH + k * P:dc * CH + (k + 1) * P],
                                         rwT[:, dc, :], start=(dc == 0), stop=(dc == DC - 1))
                last.then_inc(logit_done, 1)

            pe.wait_ge(consts_made, 1)
            pe.wait_ge(small_loaded, 16 * 6)
            for dc in range(DC):
                for ec in range(DC):
                    pe.transpose(bank[7][:, dc * D + ec * P:dc * D + (ec + 1) * P],
                                 wo[:, ec, dc * P:(dc + 1) * P], ident[:, :])
                last = pe.transpose(bank[6][:, dc * E:(dc + 1) * E], rw[:, dc * P:(dc + 1) * P],
                                    ident[0:E, 0:E])
            last.then_inc(param_T, 1)
            pe.wait_ge(param_ready, 1)
            skewed(pe, NCH, [(0, transpose_x), (2, project), (4, transpose_xs), (5, logits)], unroll=RING)

            pe.wait_ge(both_ready, 1)
            pe.wait_ge(consts_made, 2)
            both_v = both[:, :, :].rearrange("p e t -> p (e t)")
            pe.matmul(bank[5][:, 0:E * NT], from16[:, :], both_v, start=True, stop=True)
            pe.matmul(bank[4][:, 0:E * NT], ones16[:, :], both_v, start=True, stop=True).then_inc(rank_done, 1)

            for h in range(2):
                pe.wait_ge(onehot_ready, h + 1)
                for n in range(NH):
                    last = pe.matmul(bank[n % K][:, 0:NQ], row1h[h][:, :, n], col1h[h][:, :, n],
                                     start=(h == 0 and n < K), stop=(h == 1 and n >= NH - K))
            last.then_inc(onehot_used, 1)
            pe.wait_ge(wab_ready, 1)
            pe.transpose(bank[2][0:K * NT, 0:P], wab[:, :, :].rearrange("p k t -> p (k t)"), ident[:, :]
                         ).then_inc(wabT_done, 1)

            def up(j, u, half):
                e = pe.value_load(expert[0:1, bass.ds(j, 1)], min_val=0, max_val=E - 1)
                pe.wait_ge(w_ready, e * 2 + 2)
                if not isinstance(j, int) or j >= 1:
                    pe.wait_ge(gelu_done, 4 * j)
                pe.wait_ge(xgT_ready[u], 32 * (half + 1))
                for hc in range(HC):
                    o = bank[hc // 2][:, (hc % 2) * SL:(hc % 2 + 1) * SL]
                    for dc in range(DC):
                        x_hi, x_lo = xgT[u][:, dc, :], xgT[u][:, DC + dc, :]
                        w_hi = w16(0, e, dc * H + hc * P, P)
                        w_lo = w16(0, e, WE + dc * H + hc * P, P)
                        pe.matmul(o, w_hi, x_hi, start=(dc == 0), stop=False)
                        pe.matmul(o, w_hi, x_lo, start=False, stop=False)
                        last = pe.matmul(o, w_lo, x_hi, start=False, stop=(dc == DC - 1))
                    if hc % 2 == 1:
                        last.then_inc(up_done, 1)

            def down(j, u, half):
                e = pe.value_load(expert[0:1, bass.ds(j, 1)], min_val=0, max_val=E - 1)
                if not isinstance(j, int) or j >= 1:
                    pe.wait_ge(ys_ready, SUB * j)
                for hc in range(HC):
                    if hc % 2 == 0:
                        pe.wait_ge(h_ready, 4 * j + hc // 2 + 1)
                    w_hi = w16(1, e, hc * D, D)
                    w_lo = w16(1, e, WE + hc * D, D)
                    for q in range(SUB):
                        c = slice(q * P, (q + 1) * P)
                        o = bank[6 + q][:, 0:D]
                        pe.matmul(o, hh[u][:, hc, c], w_hi, start=(hc == 0), stop=False)
                        pe.matmul(o, hh[u][:, hc, c], w_lo, start=False, stop=False)
                        last = pe.matmul(o, hl[u][:, hc, c], w_hi, start=False, stop=(hc == HC - 1))
                last.then_inc(down_done, 1)

            pe.wait_ge(tables_ready, 1)
            skewed(pe, NJ, [(1, up), (2, down)], last=LAST, there=tiles_used(pe))

        @block.scalar
        def _(act):
            def square(m, e, loaded, count):
                act.wait_ge(loaded, 16 * count)
                act.wait_ge(sq_done, m * E + e)
                act.activation(junk[:, :], wbuf[m][:, bass.ds(e + 1, 1), :].rearrange("p a n -> p (a n)"),
                               ACT.Square, accum_out=sq[:, m, bass.ds(e, 1)]).then_inc(sq_done, 1)

            def square_w1(c, u, quarter):
                if u % 2 == 0:
                    e = quarter * 2 + u // 2
                    square(0, e, w1_loaded, e + 1)

            def scale_b(c, r, quarter):
                u = r % 2
                act.wait_ge(xT_done, c + 1)
                if later(c):
                    act.wait_ge(scan_done, c - 1)
                for dc in range(DC):
                    last = act.activation(bx[u][:, dc, :], bank[u][:, dc * CH:(dc + 1) * CH], ACT.Copy,
                                          scale=ab[:, 1, dc:dc + 1])
                last.then_inc(bx_done, 1)

            def deviation(c, r, quarter):
                u = r % 2
                act.wait_ge(mv_done, c + 1)
                if later(c):
                    act.wait_ge(rstd_done, c - 1)
                act.activation(std[u][:, :], mv[u][:, :, 1], ACT.Sqrt, bias=eps1[:, 0:1], scale=XS ** -2
                               ).then_inc(std_done, 1)

            def high_part(c, u, quarter):
                act.wait_ge(norm_done, c + 1)
                if later(c, RING):
                    act.wait_ge(xh_stored[u], 16 * quarter)
                act.activation(xhl[u][:, :, 0:D], xs[u], ACT.Copy).then_inc(hi_done, 1)

            def store_x(c, u, quarter):
                act.wait_ge(norm_done, c + 1)
                act.dma_start(xs_c[bass.ds(c, 1)].rearrange("a p k n -> (a p) k n"), xs[u]
                              ).then_inc(xs_stored[u], 16)
                act.wait_ge(hi_done, c + 1)
                act.wait_ge(lo_done, c + 1)
                act.dma_start(xh_c[bass.ds(c, 1)].rearrange("a p k n -> (a p) k n"), xhl[u]
                              ).then_inc(xh_stored[u], 16)

            def copy_xsT(c, r, quarter):
                u = r % 2
                act.wait_ge(t2_done, c + 1)
                if later(c):
                    act.wait_ge(logit_done, c - 1)
                act.activation(xsT[u], bank[4 + u][:, :], ACT.Copy).then_inc(xsT_done, 1)

            with nc.allow_non_contiguous_dma(reason="two vectors, one element a partition"):
                act.dma_start(ab[:, 0, :], a.rearrange("(c p) -> p c", p=P)).then_inc(small_loaded, 16)
                act.dma_start(ab[:, 1, :], b.rearrange("(c p) -> p c", p=P)).then_inc(small_loaded, 16)
            act.dma_start(wo, w_out.rearrange("(c p) d -> p c d", p=P)).then_inc(small_loaded, 16)
            act.dma_start(rw, router_w).then_inc(small_loaded, 16)
            for k in range(CT):
                act.dma_start(bout[:, k, :], b_out.partition_broadcast(P)).then_inc(small_loaded, 16)
            act.wait_ge(small_loaded, 16 * 6)
            act.dma_start(xs_rows[N:N + SL, :].rearrange("(k p) n -> p k n", p=P), bout).then_inc(dump_ready, 16)
            act.activation(th[:, :], ab[:, 0, :], ACT.Tanh).then_inc(th_ready, 1)
            act.wait_ge(param_T, 1)
            act.activation(rwT[:, :, :].rearrange("p c e -> p (c e)"), bank[6][:, 0:DC * E], ACT.Copy)
            act.activation(woT[:, :, :].rearrange("p c e -> p (c e)"), bank[7][:, :], ACT.Copy
                           ).then_inc(param_ready, 1)
            act.wait_ge(consts_made, 1)
            skewed(act, NCH, [(3, deviation), (0, scale_b), (4, high_part), (4, copy_xsT), (5, store_x),
                              (5, square_w1)], unroll=RING)

            act.wait_ge(ex_in, 1)
            act.activation(ex[:, :, :], ex[:, :, :], ACT.Exp, scale=1.0 / XS).then_inc(ex_out, 1)
            for e in range(E):
                square(1, e, w2_loaded[e % 2], e // 2 + 1)
            act.wait_ge(sqa_done, 2)
            act.activation(top[:, :], sqa[:, :], ACT.Sqrt).then_inc(top_done, 1)

            act.wait_ge(scales_ready, 1)
            act.wait_ge(dump_ready, 16)

            def split_high(e):
                for m in range(2):
                    if e:
                        act.wait_ge(w_ready, 2 * (e - 1) + m + 1)
                    act.activation(w16(m, e, 0, WE), wbuf[m][:, e + 1, :], ACT.Copy, scale=ws[:, m:m + 1]
                                   ).then_inc(whi_done, 1)

            split_high(0)

            def gelu(j, u, half):
                for q in range(4):
                    act.wait_ge(up_done, 4 * j + q + 1)
                    if not isinstance(j, int) or j >= 1:
                        act.wait_ge(h_ready, 4 * (j - 1) + q + 1)
                    act.activation(g[:, q, :], bank[q][:, :], ACT.Gelu, scale=unz[:, 0:1]
                                   ).then_inc(gelu_done, 1)

            def copy_y(j, u, half):
                act.wait_ge(down_done, j + 1)
                act.wait_ge(wsl_loaded[u], 32 * (half + 1))
                if later(j):
                    act.wait_ge(y_added, 32 * (j - 1))
                for q in range(SUB):
                    act.activation(ys[u][:, q, :], bank[6 + q][:, 0:D], ACT.Copy, scale=wsl[u][:, q:q + 1]
                                   ).then_inc(ys_ready, 1)

            split_high(1)
            act.wait_ge(route_ready, 1)
            skewed(act, NJ, [(0, gelu), (None, lambda s: split_high(s + 2)), (1, copy_y)], first=E - 2,
                   last=LAST, there=tiles_used(act))

            def f_deviation(c, u, half):
                act.wait_ge(f_mv, c + 1)
                if later(c):
                    act.wait_ge(f_rstd, c - 1)
                act.activation(fstd[u][:, :], fmv[u][:, :, 1], ACT.Sqrt, bias=eps2[:, 0:1]).then_inc(f_std, 1)

            def f_apply(c, u, half):
                apart(act, f_shift, c + 1)
                for k in range(FT - 1):
                    last = act.activation(of[:, bass.ds(c * FT + k, 1), :].rearrange("p t d -> p (t d)"),
                                          rf[:, bass.ds(c * FT + k, 1), :].rearrange("p t d -> p (t d)"),
                                          ACT.Identity, bias=fshift[u][:, k:k + 1], scale=frstd[u][:, k:k + 1])
                last.then_inc(f_out[0], 1)

            skewed(act, NF, [(0, f_deviation), (1, f_apply)], first=NF)

        @block.vector
        def _(dve):
            def scan(c, r, quarter):
                u = r % 2
                dve.wait_ge(bx_done, c + 1)
                if later(c):
                    dve.wait_ge(proj_done, c - 1)
                if u == 1:
                    dve.wait_ge(scan_done, c)
                for dc in range(DC):
                    last = dve.tensor_tensor_scan(
                        out=y[u][:, dc, :], data0=decay[:, dc, :], data1=bx[u][:, dc, :],
                        initial=0.0 if u == 0 else y[0][:, dc, CH - 1:CH], op0=ALU.mult, op1=ALU.add)
                last.then_inc(scan_done, 1)

            def add(c, r, quarter):
                u = r % 2
                dve.wait_ge(proj_done, c + 1)
                dve.wait_ge(xpb_done, c + 1)
                dve.tensor_tensor(res[u][:, :, :].rearrange("p k d -> p (k d)"), bank[2 + u][:, :],
                                  xpb[r][:, :, :].rearrange("p k d -> p (k d)"), ALU.add).then_inc(add_done, 1)

            def statistics(c, r, quarter):
                u = r % 2
                dve.wait_ge(add_done, c + 1)
                for k in range(CT):
                    last = dve.bn_stats(stats[u][:, k, :], res[u][:, k, :])
                last.then_inc(stat_done, 1)

            def aggregate(c, r, quarter):
                u = r % 2
                apart(dve, stat_done, c + 1)
                for k in range(CT):
                    last = dve.bn_aggr(mv[u][:, k, :], stats[u][:, k, :])
                last.then_inc(mv_done, 1)

            def invert(c, r, quarter):
                u = r % 2
                dve.wait_ge(std_done, c + 1)
                dve.reciprocal(rstd[u][:, :], std[u][:, :]).then_inc(rstd_done, 1)

            def normalise(c, r, quarter):
                u = r % 2
                if later(c, RING):
                    dve.wait_ge(xs_stored[r], 16 * quarter)
                    dve.wait_ge(t2_done, c - 3)
                    dve.wait_ge(lo_done, c - 3)
                dve.wait_ge(rstd_done, c + 1)
                for k in range(CT):
                    last = dve.tensor_scalar(xs[r][:, k, :], res[u][:, k, :], mv[u][:, k, 0:1],
                                             rstd[u][:, k:k + 1], ALU.subtract, ALU.mult)
                last.then_inc(norm_done, 1)

            dve.wait_ge(th_ready, 1)
            dve.wait_ge(consts_made, 1)
            for dc in range(DC):
                last = dve.tensor_scalar(decay[:, dc, :], ones_ch, th[:, dc:dc + 1], None, ALU.mult)
            last.then_inc(decay_ready, 1)
            dve.wait_ge(decay_ready, 1)
            skewed(dve, NCH, [(1, scan), (3, invert), (2, add), (3, normalise), (2, statistics), (2, aggregate)],
                   unroll=RING)

            step = [0]

            def link(ins):
                step[0] += 1
                ins.then_inc(dve_step, 1)
                dve.wait_ge(dve_step, step[0])

            def over_e(v):
                return v[:, :].unsqueeze(2).to_broadcast([P, NT, E])

            def over_t(v):
                return v[:, :].unsqueeze(2).to_broadcast([P, E, NT])

            def te(v):
                return v[:, :, :].rearrange("p e t -> p t e")

            dve.wait_ge(logit_done, NCH)
            dve.wait_ge(consts_made, 2)
            lg = bank[6][:, 0:NT * E].rearrange("p (t e) -> p t e", e=E)
            link(dve.tensor_reduce(mx[:, :], lg, AX.X, ALU.max))
            dve.tensor_tensor(ex[:, :, :], lg, over_e(mx), ALU.subtract).then_inc(ex_in, 1)

            dve.wait_ge(ex_out, 1)
            link(dve.tensor_reduce(sm[:, :], ex[:, :, :], AX.X, ALU.add))
            link(dve.reciprocal(rs[:, :], sm[:, :]))
            link(dve.tensor_tensor(pr[:, :, :], ex[:, :, :], over_e(rs), ALU.mult))
            link(dve.tensor_reduce(p1[:, :], pr[:, :, :], AX.X, ALU.max))
            link(dve.tensor_tensor(eq[:, :, :], pr[:, :, :], over_e(p1), ALU.is_equal))
            link(dve.tensor_tensor(eq[:, :, :], eq[:, :, :], rev[:, :, :], ALU.mult))
            link(dve.tensor_reduce(k1[:, :], eq[:, :, :], AX.X, ALU.max))
            link(dve.tensor_tensor(oh1[:, :, :], rev[:, :, :], over_e(k1), ALU.is_equal))
            link(dve.scalar_tensor_tensor(out=pr[:, :, :], in0=oh1[:, :, :], scalar=-4.0, in1=pr[:, :, :],
                                          op0=ALU.mult, op1=ALU.add))
            link(dve.tensor_reduce(p2[:, :], pr[:, :, :], AX.X, ALU.max))
            link(dve.tensor_tensor(eq[:, :, :], pr[:, :, :], over_e(p2), ALU.is_equal))
            link(dve.tensor_tensor(eq[:, :, :], eq[:, :, :], rev[:, :, :], ALU.mult))
            link(dve.tensor_reduce(k1[:, :], eq[:, :, :], AX.X, ALU.max))
            link(dve.tensor_tensor(oh2[:, :, :], rev[:, :, :], over_e(k1), ALU.is_equal))
            dve.tensor_tensor(te(both), oh1[:, :, :], oh2[:, :, :], ALU.add).then_inc(both_ready, 1)
            dve.wait_ge(rank_done, 1)
            link(dve.tensor_tensor_scan(out=incl[:, :, :].rearrange("p e t -> p (e t)"),
                                        data0=keep[:, :, :].rearrange("p e t -> p (e t)"),
                                        data1=bank[4][:, 0:E * NT],
                                        initial=0.0, op0=ALU.mult, op1=ALU.add))
            link(dve.tensor_copy(cnt[:, :], incl[:, :, NT - 1]))
            few = slot[:, :, 0:NT // 2]
            link(dve.tensor_tensor(few, tile_k[:, :, :], cnt[:, :].unsqueeze(2).to_broadcast([P, E, NT // 2]),
                                   ALU.is_lt))
            link(dve.tensor_reduce(nt[:, :], few, AX.X, ALU.add))
            link(dve.tensor_scalar(nt[:, :], nt[:, :], 1.0, None, ALU.max))
            link(dve.tensor_tensor_scan(out=endt[:, :], data0=one_e[:, :], data1=nt[:, :], initial=0.0,
                                        op0=ALU.mult, op1=ALU.add))
            dve.tensor_scalar(used[:, :], endt[0:1, E - 1:E], float(NJ - LAST), None, ALU.max)
            link(dve.tensor_tensor(base[:, :], endt[:, :], nt[:, :], ALU.subtract))
            link(dve.tensor_scalar(base[:, :], base[:, :], float(SL), None, ALU.mult))
            link(dve.tensor_tensor(incl[:, :, :], incl[:, :, :], over_t(base), ALU.add))
            link(dve.tensor_tensor(slot[:, :, :].rearrange("p e t -> p (e t)"), bank[5][:, 0:E * NT],
                                   incl[:, :, :].rearrange("p e t -> p (e t)"), ALU.add))
            dve.tensor_tensor(eq[:, :, :], oh1[:, :, :], te(slot), ALU.mult)
            link(dve.tensor_tensor(ex[:, :, :], oh2[:, :, :], te(slot), ALU.mult))
            dve.tensor_reduce(sl[:, 0, :], eq[:, :, :], AX.X, ALU.add)
            link(dve.tensor_reduce(sl[:, 1, :], ex[:, :, :], AX.X, ALU.add))
            link(dve.tensor_copy(sli[:, :, :], sl[:, :, :]))
            dve.tensor_scalar(slr_i[:, :, :], sli[:, :, :], P - 1, None, ALU.bitwise_and)
            link(dve.tensor_scalar(slj_i[:, :, :], sli[:, :, :], 7, None, ALU.logical_shift_right))
            tk = "p (t k) -> p k t"
            dve.tensor_copy(slr[:, :].rearrange(tk, k=K), slr_i[:, :, :])
            link(dve.tensor_copy(slj[:, :].rearrange(tk, k=K), slj_i[:, :, :]))

            dve.wait_ge(consts_made, 3)
            for h in range(2):
                def over(v, n):
                    return v.unsqueeze(1).to_broadcast([P, n, NH])

                link(dve.tensor_tensor(col1h[h], iota_r[:, 0:NQ, :], over(slj[:, h * NH:(h + 1) * NH], NQ),
                                       ALU.is_equal))
                dve.tensor_tensor(col1h[h], col1h[h], over(code[:, h, :], NQ), ALU.mult)
                dve.tensor_tensor(row1h[h], iota_r, over(slr[:, h * NH:(h + 1) * NH], P), ALU.is_equal
                                  ).then_inc(onehot_ready, 1)
                if h == 0:
                    dve.wait_ge(sq_done, 2 * E)
                    dve.tensor_reduce(sqm[:, :], sq[:, :, :], AX.X, ALU.max).then_inc(sqa_done, 1)

            dve.wait_ge(top_done, 1)
            link(dve.tensor_scalar(top[:, :], top[:, :], 2.0 ** -40, None, ALU.max))
            link(dve.tensor_scalar(pow2[:, :].bitcast(I32), top[:, :].bitcast(I32), 0x7F800000, None,
                                   ALU.bitwise_and))
            link(dve.reciprocal(ipow2[:, :], pow2[:, :]))
            link(dve.tensor_scalar(ws[:, :], ipow2[:, :], S_TOP, None, ALU.mult))
            dve.tensor_scalar(unz[:, :], pow2[:, 0:1], 1.0 / (S_TOP * XS), None, ALU.mult)
            link(dve.tensor_scalar(hs[:, :], ipow2[:, 0:1], S_TOP / 256, None, ALU.mult))
            dve.scalar_tensor_tensor(out=uny[:, :], in0=pow2[:, 0:1], scalar=256 * XS / S_TOP ** 2,
                                     in1=pow2[:, 1:2], op0=ALU.mult, op1=ALU.mult).then_inc(scales_ready, 1)

            link(dve.tensor_tensor(sm[:, :], p1[:, :], p2[:, :], ALU.add))
            link(dve.reciprocal(rs[:, :], sm[:, :]))
            link(dve.tensor_scalar(rs[:, :], rs[:, :], uny[:, 0:1], None, ALU.mult))
            dve.tensor_tensor(wab[:, 0, :], p1[:, :], rs[:, :], ALU.mult)
            dve.tensor_tensor(wab[:, 1, :], p2[:, :], rs[:, :], ALU.mult).then_inc(wab_ready, 1)

            def split_low(e):
                for m in range(2):
                    dve.wait_ge(whi_done, 2 * e + m + 1)
                    dve.scalar_tensor_tensor(out=w16(m, e, WE, WE), in0=wbuf[m][:, e + 1, :],
                                             scalar=ws[:, m:m + 1], in1=w16(m, e, 0, WE),
                                             op0=ALU.mult, op1=ALU.subtract).then_inc(w_ready, 1)

            dve.wait_ge(onehot_used, 1)
            link(dve.tensor_copy(v0[:, :], bank[0][:, 0:NQ]))
            dve.tensor_scalar(vk[:, :], bank[1][:, 0:NQ], 0.0, float(N), ALU.not_equal, ALU.mult)
            link(dve.tensor_tensor(vs[:, :], bank[1][:, 0:NQ], v0[:, :], ALU.add))
            dve.tensor_scalar(vneg[:, :], vs[:, :], 0.0, float(N // 2), ALU.is_lt, ALU.mult)
            dve.scalar_tensor_tensor(out=v0[:, :], in0=vs[:, :], scalar=0.0, in1=dump[:, :],
                                     op0=ALU.is_equal, op1=ALU.mult)
            link(dve.scalar_tensor_tensor(out=va[:, :], in0=vs[:, :], scalar=-1.0, in1=vs[:, :],
                                          op0=ALU.mult, op1=ALU.max))
            link(dve.tensor_tensor(va[:, :], va[:, :], vneg[:, :], ALU.add))
            link(dve.tensor_scalar(tok[:, :], va[:, :], -1.0, 0.0, ALU.add, ALU.max))
            dve.tensor_copy(idx[:, 0, :], tok[:, :])
            dve.tensor_tensor(idx[:, 1, :], tok[:, :], vk[:, :], ALU.add)
            dve.tensor_tensor(idx[:, 2, :], tok[:, :], v0[:, :], ALU.add).then_inc(route_ready, 1)

            link(dve.tensor_tensor(past[:, :, :], iota_j[0:1, :, :],
                                   endt[0:1, :].unsqueeze(1).to_broadcast([1, NJ, E]), ALU.is_ge))
            link(dve.tensor_reduce(expf[:, :], past[:, :, :], AX.X, ALU.add))
            dve.tensor_scalar(expert[:, 0:NJ], expf[:, :], float(E - 1), None, ALU.min).then_inc(tables_ready, 1)

            dve.wait_ge(wabT_done, 1)
            dve.tensor_copy(wabT[:, :], bank[2][0:K * NT, 0:P]).then_inc(wabT_ready, 1)

            split_low(0)

            def split(j, u, half):
                if later(j):
                    dve.wait_ge(down_done, j - 1)
                for q in range(4):
                    hi = hh[u][:, 2 * q:2 * q + 2, :].rearrange("p c s -> p (c s)")
                    lo = hl[u][:, 2 * q:2 * q + 2, :].rearrange("p c s -> p (c s)")
                    dve.wait_ge(gelu_done, 4 * j + q + 1)
                    dve.tensor_scalar(hi, g[:, q, :], hs[:, 0:1], None, ALU.mult).then_inc(hh_done, 1)
                    dve.wait_ge(hh_done, 4 * j + q + 1)
                    dve.scalar_tensor_tensor(out=lo, in0=g[:, q, :], scalar=hs[:, 0:1], in1=hi,
                                             op0=ALU.mult, op1=ALU.subtract).then_inc(h_ready, 1)

            skewed(dve, NJ, [(1, split), (None, lambda s: split_low(s + 1))], first=E - 1,
                   last=LAST, there=tiles_used(dve))

            def f_statistics(c, u, half):
                apart(dve, f_loaded[u], 16 * (half + 1))
                if later(c):
                    apart(dve, f_std, c - 1)
                for k in range(FT):
                    last = dve.bn_stats(fstats[u][:, k, :],
                                        rf[:, bass.ds(c * FT + k, 1), :].rearrange("p t d -> p (t d)"))
                last.then_inc(f_stat, 1)
                apart(dve, f_stat, c + 1)
                if later(c):
                    dve.wait_ge(f_shift, c - 1)
                    dve.wait_ge(f_out[1], c - 1)
                for k in range(FT):
                    last = dve.bn_aggr(fmv[u][:, k, :], fstats[u][:, k, :])
                last.then_inc(f_mv, 1)

            def f_scale(c, u, half):
                dve.wait_ge(f_std, c + 1)
                if later(c):
                    for by in f_out:
                        dve.wait_ge(by, c - 1)
                dve.reciprocal(frstd[u][:, :], fstd[u][:, :]).then_inc(f_rstd, 1)
                dve.wait_ge(f_rstd, c + 1)
                dve.scalar_tensor_tensor(out=fshift[u][:, :], in0=fmv[u][:, :, 0], scalar=-1.0,
                                         in1=frstd[u][:, :], op0=ALU.mult, op1=ALU.mult).then_inc(f_shift, 1)

            skewed(dve, NF, [(0, f_statistics), (1, f_scale)], first=NF)


_INS = ["L0_attn_x", "L0_attn_a", "L0_attn_b", "L0_attn_w_out", "L0_attn_b_out", "L0_ffn_router_w", "L0_ffn_w1",
        "L0_ffn_w2"]


def kernel(**inputs):
    import numpy as np
    import concourse.bacc as bacc
    from concourse.bass_utils import run_bass_kernel_spmd

    nc = bacc.Bacc("TRN2", target_bir_lowering=False, num_devices=1)
    arrays, args = {}, []
    for name in _INS:
        v = np.ascontiguousarray(inputs[name])
        arrays[name] = v
        args.append(nc.dram_tensor(name, v.shape, mybir.dt.from_np(v.dtype), kind="ExternalInput").ap())
    B, S, D = inputs["L0_attn_x"].shape
    args.append(nc.dram_tensor("out", (B, S, D), F32, kind="ExternalOutput").ap())
    args.append(nc.dram_tensor("xh_rows", (B * S, 2 * D), F16, kind="Internal").ap())
    args.append(nc.dram_tensor("xs_rows", (B * S + 256, D), F32, kind="Internal").ap())
    args.append(nc.dram_tensor("w_rows", (2 * B * S, 1), F32, kind="Internal").ap())
    build(nc, *args)
    r = run_bass_kernel_spmd(nc, [arrays], core_ids=[0])
    return r.results[0]["out"]
```
